# Optimizing a Trainium2 kernel written in Bass

```python
import numpy as np
import jax
import jax.numpy as jnp

def _softmax(x, axis=-1):
    return jax.nn.softmax(x, axis=axis)
def _gelu(x):
    return jax.nn.gelu(x, approximate=True)
def _silu(x):
    return jax.nn.silu(x)
def _sigmoid(x):
    return jax.nn.sigmoid(x)
def _layernorm(x, axis=-1, eps=1e-5):
    m = jnp.mean(x, axis=axis, keepdims=True)
    v = jnp.var(x, axis=axis, keepdims=True)
    return (x - m) / jnp.sqrt(v + eps)
def _scatter_add(tgt, idx, src, axis=0):
    return tgt.at[idx].add(src)
def _segment_sum(src, seg, n):
    return jax.ops.segment_sum(src, seg, n)

kernel_name = 'mk_adj_preln_d2_adj_256_b74c3b'

def setup_inputs(seed: int = 0):
    np.random.seed(seed)
    _w = jnp.asarray
    def _rec_inputs():
        import jax
        import jax.numpy as jnp
        _gk = jax.random.key(seed)
        x = -0.0005207 + 1.001 * jax.random.normal(jax.random.fold_in(_gk, 1), (8, 2048, 256), jnp.float32)
        _w = (1.0 + jnp.arange(2048, dtype=jnp.float32)) ** -0.5
        _w = _w / _w.mean()
        _pij = jnp.clip(0.0078125 * _w[:, None] * _w[None, :], 0.0, 1.0)
        _a = jax.random.uniform(jax.random.fold_in(_gk, 2), (2048, 2048)) < _pij
        adj = _a.astype(jnp.int32)
        return x, adj
    x, adj = _rec_inputs()
    def _L0_gnn_setup():
        import jax, jax.numpy as jnp
        import numpy as np
        import math
        CHUNK = 256
        NUM_HEADS = 4
        EPS = 1e-05
        key = jax.random.key(seed)
        ks = jax.random.split(key, 12)
        B, N, F = (4, 2048, 256)
        x = jax.random.normal(ks[0], (B, N, F), dtype=jnp.float32)
        adj_matrix = jax.random.randint(ks[1], (N, N), 0, 2, dtype=jnp.int32)
        s = 1.0 / math.sqrt(F)
        Wq = jax.random.normal(ks[2], (F, F), dtype=jnp.float32) * s
        bq = jnp.zeros((F,), dtype=jnp.float32)
        Wk = jax.random.normal(ks[3], (F, F), dtype=jnp.float32) * s
        bk = jnp.zeros((F,), dtype=jnp.float32)
        Wv = jax.random.normal(ks[4], (F, F), dtype=jnp.float32) * s
        bv = jnp.zeros((F,), dtype=jnp.float32)
        Wo = jax.random.normal(ks[5], (F, F), dtype=jnp.float32) * s
        bo = jnp.zeros((F,), dtype=jnp.float32)
        gamma = jnp.ones((F,), dtype=jnp.float32)
        beta = jnp.zeros((F,), dtype=jnp.float32)
        return {'x': x, 'adj_matrix': adj_matrix, 'Wq': Wq, 'bq': bq, 'Wk': Wk, 'bk': bk, 'Wv': Wv, 'bv': bv, 'Wo': Wo, 'bo': bo, 'gamma': gamma, 'beta': beta}
    _L0_gnn_all = _L0_gnn_setup()
    _L0_gnn_in = {k: v for k, v in _L0_gnn_all.items() if k in ('Wq', 'bq', 'Wk', 'bk', 'Wv', 'bv', 'Wo', 'bo', 'gamma', 'beta', )}
    del _L0_gnn_all

    def _L1_gnn_setup():
        import jax, jax.numpy as jnp
        import numpy as np
        ALPHA = 0.2
        MASK_VAL = -9000000000000000.0
        key = jax.random.key(seed)
        k1, k2, k3, k4 = jax.random.split(key, 4)
        B, N, F = (8, 1024, 256)
        H, OUT = (4, 256)
        hs = OUT // H
        x = jax.random.normal(k1, (B, N, F), dtype=jnp.float32)
        adj = jax.random.randint(k2, (N, N), 0, 2, dtype=jnp.int32)
        wb = float(np.sqrt(6.0 / (F + hs)))
        ab = float(np.sqrt(6.0 / (H + 2 * hs)))
        W = jax.random.uniform(k3, (H, F, hs), dtype=jnp.float32, minval=-wb, maxval=wb)
        a = jax.random.uniform(k4, (H, 2 * hs), dtype=jnp.float32, minval=-ab, maxval=ab)
        return {'x': x, 'adj': adj, 'W': W, 'a': a}
    _L1_gnn_all = _L1_gnn_setup()
    _L1_gnn_in = {k: v for k, v in _L1_gnn_all.items() if k in ('W', 'a', )}
    del _L1_gnn_all

    return {
        "x": x,
        "adj": adj,
        "L0_gnn_Wq": _L0_gnn_in["Wq"],
        "L0_gnn_bq": _L0_gnn_in["bq"],
        "L0_gnn_Wk": _L0_gnn_in["Wk"],
        "L0_gnn_bk": _L0_gnn_in["bk"],
        "L0_gnn_Wv": _L0_gnn_in["Wv"],
        "L0_gnn_bv": _L0_gnn_in["bv"],
        "L0_gnn_Wo": _L0_gnn_in["Wo"],
        "L0_gnn_bo": _L0_gnn_in["bo"],
        "L0_gnn_gamma": _L0_gnn_in["gamma"],
        "L0_gnn_beta": _L0_gnn_in["beta"],
        "L1_gnn_W": _L1_gnn_in["W"],
        "L1_gnn_a": _L1_gnn_in["a"],
    }

def reference(x, adj, L0_gnn_Wq, L0_gnn_bq, L0_gnn_Wk, L0_gnn_bk, L0_gnn_Wv, L0_gnn_bv, L0_gnn_Wo, L0_gnn_bo, L0_gnn_gamma, L0_gnn_beta, L1_gnn_W, L1_gnn_a):
    import jax
    import jax.numpy as jnp
    def _L0_gnn_ref(x, adj_matrix, Wq, bq, Wk, bk, Wv, bv, Wo, bo, gamma, beta):
        import jax, jax.numpy as jnp
        import numpy as np
        import math
        CHUNK = 256
        NUM_HEADS = 4
        EPS = 1e-05
        B, N, Fin = x.shape
        H = NUM_HEADS
        Dout = Wq.shape[0]
        Dh = Dout // H
        Nc = N // CHUNK
        q = (x @ Wq.T + bq).reshape(B, N, H, Dh).transpose(0, 2, 1, 3)
        k = (x @ Wk.T + bk).reshape(B, N, H, Dh).transpose(0, 2, 1, 3)
        v = (x @ Wv.T + bv).reshape(B, N, H, Dh).transpose(0, 2, 1, 3)
        kc = k.reshape(B, H, Nc, CHUNK, Dh)
        vc = v.reshape(B, H, Nc, CHUNK, Dh)
        scores = jnp.einsum('bhnd,bhjcd->bhnjc', q, kc) / jnp.sqrt(jnp.asarray(Dh, dtype=q.dtype))
        scores = jnp.clip(scores, -10.0, 10.0)
        mask = adj_matrix.reshape(N, Nc, CHUNK)[None, None]
        scores = jnp.where(mask == 0, jnp.asarray(-10.0, scores.dtype), scores)
        attn = jax.nn.softmax(scores, axis=-1)
        ctx = jnp.einsum('bhnjc,bhjcd->bhnd', attn, vc)
        ctx = ctx.transpose(0, 2, 1, 3).reshape(B, N, Dout)
        out = ctx @ Wo.T + bo
        out = out + x
        mu = jnp.mean(out, axis=-1, keepdims=True)
        var = jnp.mean(jnp.square(out - mu), axis=-1, keepdims=True)
        out = (out - mu) * jax.lax.rsqrt(var + EPS) * gamma + beta
        return out

    def _L1_gnn_ref(x, adj, W, a):
        import jax, jax.numpy as jnp
        import numpy as np
        ALPHA = 0.2
        MASK_VAL = -9000000000000000.0
        B, N, _ = x.shape
        H, _, hs = W.shape
        Wh = jnp.einsum('bnf,hfd->bhnd', x, W)
        a1, a2 = (a[:, :hs], a[:, hs:])
        ei = jnp.einsum('bhnd,hd->bhn', Wh, a1)
        ej = jnp.einsum('bhnd,hd->bhn', Wh, a2)
        e = ei[:, :, :, None] + ej[:, :, None, :]
        e = jnp.where(e > 0, e, ALPHA * e)
        e = jnp.where(adj[None, None] > 0, e, MASK_VAL)
        att = jax.nn.softmax(e, axis=-1)
        h = jnp.einsum('bhij,bhjd->bhid', att, Wh)
        h = h.transpose(0, 2, 1, 3).reshape(B, N, H * hs)
        return jax.nn.elu(h)

    h = jnp.maximum(_layernorm(x, axis=-1), 0.0)
    x = x + _L0_gnn_ref(h, adj, L0_gnn_Wq, L0_gnn_bq, L0_gnn_Wk, L0_gnn_bk, L0_gnn_Wv, L0_gnn_bv, L0_gnn_Wo, L0_gnn_bo, L0_gnn_gamma, L0_gnn_beta)
    h = jnp.maximum(_layernorm(x, axis=-1), 0.0)
    x = x + _L1_gnn_ref(h, adj, L1_gnn_W, L1_gnn_a)
    return x


_drawn_inputs = setup_inputs


def setup_inputs(seed=0):
    import zlib

    import numpy as np

    out = dict(_drawn_inputs(seed))
    spreads = {'L0_gnn_bq': (0.0, 0.8),
     'L0_gnn_bk': (0.0, 0.8),
     'L0_gnn_bv': (0.0, 0.1),
     'L0_gnn_bo': (0.0, 0.414),
     'L0_gnn_gamma': (1.0, 0.2),
     'L0_gnn_beta': (0.0, 0.1)}
    factors = {}
    for name, (base, spread) in spreads.items():
        noise = np.random.default_rng([zlib.crc32(name.encode()), seed]).standard_normal(out[name].shape)
        drawn = base * np.exp(spread * noise) if base else spread * noise
        out[name] = jnp.asarray(drawn.astype(out[name].dtype))
    for name, factor in factors.items():
        out[name] = (out[name] * factor).astype(out[name].dtype)
    return out
```

```python
from contextlib import ExitStack

import concourse.bass as bass
from concourse import mybir

F32 = mybir.dt.float32
F32R = mybir.dt.float32r
BF16 = mybir.dt.bfloat16
I8 = mybir.dt.int8
I32 = mybir.dt.int32
ALU = mybir.AluOpType
ACT = mybir.ActivationFunctionType
AX = mybir.AxisListType

P = 128
B, N, F = 8, 2048, 256
H, DH = 4, 64
KC = F // P
NT = N // P
IB = 512
NI = N // IB
TI = IB // P
CH = 256
NC = N // CH
LIM = 10.0
EPS = 1e-5
ALPHA = 0.2


def pass_waits(e, sem):
    e.sem_inc(sem, 1)


class Scope:

    def __init__(self, nc):
        self.nc, self.stack = nc, ExitStack()

    def sb(self, name, shape, dt=F32):
        return self.stack.enter_context(self.nc.sbuf_tensor(name, shape, dt))

    def ps(self, name, shape, dt=F32):
        return self.stack.enter_context(self.nc.psum_tensor(name, shape, dt))

    def sem(self, name):
        return self.stack.enter_context(self.nc.semaphore(name))

    def close(self):
        self.stack.close()


def stage_prepare(nc, d, ident, mask_log):
    s = Scope(nc)
    identb = s.sb("identb", [P, P], BF16)
    eps = s.sb("a_eps", [P, 1])
    minus20 = s.sb("minus20", [P, 1])
    bo_row = s.sb("bo_row", [P, F])
    xt = s.sb("xt", [P, 2, NT, F])
    hs = s.sb("hs", [P, NT, F])
    hb = s.sb("hb", [P, NT, F])
    hT = s.sb("hT", [P, KC, N])
    stats = s.sb("stats", [P, NT, 6])
    mv = s.sb("mv", [P, NT, 2])
    sd = s.sb("sd", [P, NT])
    rs = s.sb("rs", [P, NT])
    nb = s.sb("nb", [P, NT])
    adjt = s.sb("adjt", [P, 2, N], I32)
    edge20 = s.sb("edge20", [P, N], BF16)
    code = s.sb("code", [P, N], BF16)
    mask01 = s.sb("mask01", [P, NT, N], I8)
    ps_h = s.ps("ps_h", [P, KC, IB])
    HALF = NT // 2
    ps_m = s.ps("ps_m", [P, 2, HALF, P], BF16)

    consts, xload, passed = s.sem("a_consts"), s.sem("a_x"), s.sem("a_passed")
    adj_in = (s.sem("a_adj0"), s.sem("a_adj1"))
    setup, statd, aggrd, sdd, rsd, nbd = (s.sem("a_" + n) for n in ("setup", "stat", "aggr", "sd", "rs", "nb"))
    h_made, hb_made, h_turned, h_saved = (s.sem("a_" + n) for n in ("h", "hb", "hturn", "hsave"))
    hT_out, hb_out, m_out = (s.sem("a_" + n) for n in ("hTo", "hbo", "mo"))
    edged, coded, m_turned, log_made, m01_made = (s.sem("a_" + n) for n in ("edge", "code", "mt", "log", "m01"))

    def itile(b, k):
        return bass.ds((b * 2 + k) * P, P)

    with nc.Block() as block:

        @block.sync
        def _(sp):
            def load_adj(b):
                sp.wait_ge(xload, 16)
                for k in range(2):
                    sp.dma_start(adjt[:, k, :], d["adj"][itile(b, k), :]).then_inc(adj_in[k], 16)

            def load_x(b):
                if not isinstance(b, int):
                    pass_waits(sp, passed)
                sp.dma_start(xt[:, b % 2], d["x"][b].rearrange("(t p) f -> p t f", p=P)).then_inc(xload, 16)

            def store(b):
                sp.wait_ge(h_saved, b * (2 * NI) + 2 * NI)
                pass_waits(sp, passed)
                sp.dma_start(d["hT"][b], hT[:, :, :]).then_inc(hT_out, 16)
                sp.wait_ge(hb_made, b + 1)
                pass_waits(sp, passed)
                sp.dma_start(d["hb"][b].rearrange("(t p) f -> p t f", p=P), hb[:, :, :]).then_inc(hb_out, 16)

            load_x(0)
            sp.dma_start(ident[:, :], d["ident"]).then_inc(consts, 16)
            sp.dma_start(bo_row[:, :], d["bo"].partition_broadcast(P)).then_inc(consts, 16)
            load_adj(0)
            sp.wait_ge(xload, 16)
            load_x(1)
            with sp.Fori(0, B - 2) as b:
                sp.wait_ge(coded, b * 2 + 2)
                load_adj(b + 1)
                sp.wait_ge(h_made, b * NT + NT)
                pass_waits(sp, passed)
                sp.wait_ge(xload, b * 16 + 32)
                load_x(b + 2)
                store(b)
            sp.wait_ge(coded, (B - 1) * 2)
            load_adj(B - 1)
            store(B - 2)
            store(B - 1)
            sp.wait_ge(m01_made, 4 * B)
            sp.dma_start(d["mask01"], mask01[:, :, :]).then_inc(m_out, 16)
            sp.wait_ge(m_out, 16)
            sp.wait_ge(hT_out, 16 * B)
            sp.wait_ge(hb_out, 16 * B)

        @block.vector
        def _(dve):
            dve.memset(eps[:, :], EPS).then_inc(setup, 1)
            dve.memset(minus20[:, :], -20.0).then_inc(setup, 1)
            dve.wait_ge(consts, 32)
            dve.tensor_copy(identb[:, :], ident[:, :]).then_inc(setup, 1)
            with dve.Fori(0, B) as b:
                dve.wait_ge(xload, b * 16 + 16)
                dve.wait_ge(aggrd, b * NT)
                pass_waits(dve, passed)
                for t in range(NT):
                    dve.bn_stats(stats[:, t, :], xt[:, b % 2, t, :]).then_inc(statd, 1)
                dve.wait_ge(statd, b * NT + NT)
                dve.wait_ge(nbd, b)
                dve.wait_ge(sdd, b)
                pass_waits(dve, passed)
                for t in range(NT):
                    dve.bn_aggr(mv[:, t, :], stats[:, t, :]).then_inc(aggrd, 1)
                dve.wait_ge(sdd, b + 1)
                dve.wait_ge(h_made, b * NT)
                dve.reciprocal(rs[:, :], sd[:, :]).then_inc(rsd, 1)
                dve.wait_ge(rsd, b + 1)
                dve.scalar_tensor_tensor(out=nb[:, :], in0=mv[:, :, 0], scalar=-1.0, in1=rs[:, :],
                                         op0=ALU.mult, op1=ALU.mult).then_inc(nbd, 1)
                for k in range(2):
                    dve.wait_ge(adj_in[k], b * 16 + 16)
                    dve.wait_ge(coded, b * 2 + k)
                    dve.tensor_scalar(edge20[:, :], adjt[:, k, :], 0, 20.0, ALU.not_equal, ALU.mult).then_inc(edged, 1)
                    dve.wait_ge(edged, b * 2 + k + 1)
                    dve.wait_ge(m_turned, b * 4 + 2 * k)
                    dve.scalar_tensor_tensor(out=code[:, :], in0=adjt[:, k, :], scalar=0, in1=edge20[:, :],
                                             op0=ALU.is_gt, op1=ALU.add).then_inc(coded, 1)
                    for half in range(2):
                        dve.wait_ge(m_turned, b * 4 + 2 * k + half + 1)
                        dve.tensor_scalar(mask_log[:, half * HALF:(half + 1) * HALF, itile(b, k)], ps_m[:, half],
                                          20.0, -LIM, ALU.min, ALU.add).then_inc(log_made, 1)

        @block.scalar
        def _(act):
            act.wait_ge(setup, 3)
            with act.Fori(0, B) as b:
                act.wait_ge(aggrd, b * NT + NT)
                act.wait_ge(rsd, b)
                nc.scalar.activation(sd[:, :], mv[:, :, 1], ACT.Sqrt, bias=eps[:, 0:1]).then_inc(sdd, 1)
                act.wait_ge(nbd, b + 1)
                act.wait_ge(h_turned, b * (2 * NI))
                act.wait_ge(hb_made, b)
                for t in range(NT):
                    nc.scalar.activation(hs[:, t, :], xt[:, b % 2, t, :], ACT.Relu, bias=nb[:, t:t + 1],
                                         scale=rs[:, t:t + 1]).then_inc(h_made, 1)
                act.wait_ge(hT_out, b * 16)
                for q in range(NI):
                    for kc in range(KC):
                        act.wait_ge(h_turned, b * (2 * NI) + 2 * q + kc + 1)
                        nc.scalar.copy(hT[:, kc, q * IB:(q + 1) * IB], ps_h[:, kc, :]).then_inc(h_saved, 1)
                for k in range(2):
                    for half in range(2):
                        act.wait_ge(log_made, b * 4 + 2 * k + half + 1)
                        nc.scalar.activation(mask01[:, half * HALF:(half + 1) * HALF, itile(b, k)], ps_m[:, half],
                                             ACT.Relu, bias=minus20[:, 0:1]).then_inc(m01_made, 1)

        @block.tensor
        def _(pe):
            pe.wait_ge(consts, 32)
            pe.wait_ge(setup, 3)
            with pe.Fori(0, B) as b:
                for q in range(NI):
                    pe.wait_ge(h_made, b * NT + TI * q + TI)
                    for kc in range(KC):
                        pe.wait_ge(h_saved, b * (2 * NI) + (2 * (q - 1) + kc + 1 if q else 0))
                        for t in range(TI):
                            mm = pe.transpose(ps_h[:, kc, t * P:(t + 1) * P],
                                              hs[:, q * TI + t, kc * P:(kc + 1) * P], ident[:, :])
                        mm.then_inc(h_turned, 1)
                for k in range(2):
                    pe.wait_ge(coded, b * 2 + k + 1)
                    for half in range(2):
                        last = b * 4 + (half + 1 if k else 0)
                        pe.wait_ge(log_made, last)
                        pe.wait_ge(m01_made, last)
                        for j in range(HALF):
                            jt = half * HALF + j
                            mm = pe.transpose(ps_m[:, half, j, :], code[:, jt * P:(jt + 1) * P], identb[:, :])
                        mm.then_inc(m_turned, 1)

        @block.gpsimd
        def _(pool):
            pool.wait_ge(consts, 32)
            with pool.Fori(0, B) as b:
                pool.wait_ge(h_made, b * NT + NT)
                pool.wait_ge(hb_out, b * 16)
                nc.gpsimd.tensor_tensor(hb[:, :, :], hs[:, :, :], bo_row[:, :].unsqueeze(1).broadcast_to([P, NT, F]),
                                        ALU.add).then_inc(hb_made, 1)
    s.close()


LEAD = 2
ER = 4
TPC = CH // P
UNITS_B = NC
RB_STEPS = {3: (0, 1), 4: (2, 3), 5: (4, 5), 6: (6, 7)}
RE = P // (2 * NC)
K_STEP, Q_STEP, V_STEP = 0, 2, 5


def stage_attend(nc, d, ident, mask_log):
    s = Scope(nc)
    wqT, wkT, wvT = (s.sb(n, [P, KC, F]) for n in ("wqT", "wkT", "wvT"))
    bq, bk = s.sb("bq", [P, KC]), s.sb("bk", [P, KC])
    bv = s.sb("bv", [P, F])
    onehot = s.sb("onehot", [P, 4, 32])
    sel = s.sb("sel", [4 * NC, NC, P], F32R)
    hkv = s.sb("hkv", [P, KC, IB])
    hq = s.sb("hq", [P, KC, IB])
    kst = s.sb("kst", [P, KC, 2, N], F32R)
    qst = s.sb("qst", [P, 2, 2, 2, IB], F32R)
    vt = s.sb("vt", [P, KC, NT, P])
    ex = s.sb("ex", [P, ER, TPC, 2, IB])
    pair_sum = s.sb("pair_sum", [P, ER, 2, IB])
    num = s.sb("num", [P, 2, NC, IB])
    wrow = num[:, 0, 0, :].rearrange("p (c f) -> p c f", c=KC)
    sel_in = num[0:4 * NC, 0, 1:3, :].rearrange("p a (b e) -> p (a b) e", e=P)
    den = s.sb("den_rows", [P, IB])
    den_t = s.sb("den_t", [P, IB // RE])
    rec_t = s.sb("rec_t", [P, 2, IB // RE], F32R)
    rec = s.sb("rec", [2 * 2 * NC, IB], F32R)
    ctx = s.sb("ctx", [P, IB])

    ps_s = s.ps("ps_s", [P, 2, TPC, IB])
    ps_n = s.ps("ps_n", [P, IB])
    ps_d = s.ps("ps_d", [P, IB])
    ps_r = s.ps("ps_r", [P, IB])
    ps_p = s.ps("ps_p", [P, IB])

    def sems(*names):
        return [s.sem("b_" + n) for n in names]

    w_in, small_in, w_turned, w_saved, sel_made = sems("w", "small", "wt", "ws", "selm")
    kv_in, q_in = sems("kvin", "qin")
    k_proj, q_proj, v_proj, k_hi, q_hi, k_done, q_done, v_done = sems(
        "kproj", "qproj", "vproj", "khi", "qhi", "kdone", "qdone", "vdone")
    scores, clipped, probs, summed = sems("scores", "clip", "probs", "summed")
    num_done, num_saved, den_done, den_saved, den_moved = sems("num", "nsave", "den", "dsave", "dmove")
    inverted, rec_hi, rec_lo, rec_moved, q_twice = sems("inv", "rhi", "rlo", "rmove", "qtwice")
    spread, scaled, added, ctx_out = sems("spread", "scaled", "added", "ctxout")
    bias_made, passed = sems("bias", "passed")
    NBLK = B * KC * NI

    def iterations(e, body):
        def turn(b, pair, refill, last, peel=False):
            base = b * (2 * NI) + pair * NI
            if peel:
                body(e, b, base, base, 0, pair, True, False, refill, True)
            with e.Fori(1 if peel else 0, NI - 1) as ib:
                body(e, b, base, base + ib, ib, pair, False, False, refill, True)
            body(e, b, base, base + NI - 1, NI - 1, pair, False, True, refill, not last)
        turn(0, 0, True, False, peel=True)
        turn(0, 1, True, False)
        with e.Fori(1, B - 1) as b:
            turn(b, 0, True, False)
            turn(b, 1, True, False)
        turn(B - 1, 0, True, False)
        turn(B - 1, 1, False, True)

    def cols(ib):
        return bass.ds(ib * IB, IB)

    def num_slot(it, c):
        return num[:, it % 2, c, :]

    def half(h):
        return slice(h * DH, (h + 1) * DH)

    with nc.Block() as block:

        @block.sync
        def _(sp):
            for dst, src in ((bq[:, :], d["bq"].rearrange("(c p) -> p c", p=P)),
                             (bk[:, :], d["bk"].rearrange("(c p) -> p c", p=P)),
                             (bv[:, :], d["bv"].partition_broadcast(P)),
                             (onehot[:, :, :], d["onehot"]), (sel_in[:, :, :], d["sel"])):
                sp.dma_start(dst, src, allow_slow_non_contiguous=True).then_inc(small_in, 16)
            for m, w in enumerate(("wq", "wk", "wv")):
                if m:
                    sp.wait_ge(w_turned, 2 * m)
                sp.dma_start(wrow[:, :, :], d[w].rearrange("(c p) f -> p c f", p=P)).then_inc(w_in, 16)

            def load(dst, b, ib, sem):
                sp.dma_start(dst, d["hT"][b][:, :, cols(ib)]).then_inc(sem, 16)

            load(hq[:, :, :], 0, 0, q_in)
            for ib in range(NI):
                if ib:
                    sp.wait_ge(v_proj, ib)
                load(hkv[:, :, :], 0, ib, kv_in)

            def queries_twice(it, par):
                sp.wait_ge(q_done, it + 1)
                for h in range(2):
                    sp.dma_start(qst[half(1 - h), par, h].bitcast(F32), qst[half(h), par, h].bitcast(F32)).then_inc(q_twice, 16)

            def gather(it):
                sp.wait_ge(den_saved, it + 1)
                for q in range(4):
                    sp.dma_start(den_t[q * 32:(q + 1) * 32, :], den[q * 32:q * 32 + NC // 2, :].rearrange(
                        "m (i e) -> m i e", i=RE)).then_inc(den_moved, 16)

            def scatter(it):
                sp.wait_ge(rec_lo, it + 1)
                sp.wait_ge(spread, it * NC)
                for k in range(2):
                    sp.dma_start(rec[k * 2 * NC:(k + 1) * 2 * NC, :].bitcast(F32).rearrange("r (i e) -> r i e", i=RE),
                                 rec_t[:, k, :].bitcast(F32)).then_inc(rec_moved, 16)

            sp.wait_ge(v_proj, NI)
            load(hkv[:, :, :], 0, 0, kv_in)
            queries_twice(0, 0)

            def body(e, b, base, it, ib, pair, first, cross, refill, more):
                if not first:
                    gather(it - 1)
                if more:
                    sp.wait_ge(q_proj, it + 1)
                    pass_waits(sp, passed)
                    nb_, nib = (b + pair, 0) if cross else (b, ib + 1)
                    load(hq[:, :, :], nb_, nib, q_in)
                if not first:
                    scatter(it - 1)
                if more:
                    queries_twice(it + 1, (it + 1) % 2)
                if refill and not (cross and isinstance(b, int) and b == B - 1):
                    sp.wait_ge(v_proj, it + NI + 1)
                    rb, rib = (b + 1, 0) if cross else (b + pair, ib + 1)
                    load(hkv[:, :, :], rb, rib, kv_in)
                if not first:
                    sp.wait_ge(added, it * (NC - 1))
                    sp.dma_start(d["ctxT"][it - 1], ctx[:, :]).then_inc(ctx_out, 16)

            iterations(sp, body)
            gather(NBLK - 1)
            scatter(NBLK - 1)
            sp.wait_ge(added, NBLK * (NC - 1))
            sp.dma_start(d["ctxT"][NBLK - 1], ctx[:, :]).then_inc(ctx_out, 16)
            sp.wait_ge(ctx_out, 16 * NBLK)

        @block.tensor
        def _(pe):
            pe.wait_ge(small_in, 16 * 5)
            for m in range(3):
                pe.wait_ge(w_in, 16 * (m + 1))
                if m:
                    pe.wait_ge(w_saved, m)
                for kc in range(KC):
                    for oc in range(KC):
                        mm = pe.transpose(ps_s[:, 0, kc, oc * P:(oc + 1) * P], wrow[:, oc, kc * P:(kc + 1) * P],
                                          ident[:, :])
                    mm.then_inc(w_turned, 1)

            def project_k(pair, n):
                pe.wait_ge(kv_in, n * 16 + 16)
                pe.wait_ge(v_done, n)
                for kc in range(KC):
                    mm = pe.matmul(ps_p[:, :], wkT[:, kc, pair * P:(pair + 1) * P], hkv[:, kc, :],
                                   start=(kc == 0), stop=(kc == KC - 1))
                mm.then_inc(k_proj, 1)

            def project_v(pair, n):
                for t in range(TI):
                    for kc in range(KC):
                        mm = pe.matmul(ps_p[:, t * P:(t + 1) * P], hkv[:, kc, t * P:(t + 1) * P],
                                       wvT[:, kc, pair * P:(pair + 1) * P], start=(kc == 0), stop=(kc == KC - 1))
                mm.then_inc(v_proj, 1)

            def project_q(pair, nit):
                pe.wait_ge(q_in, nit * 16 + 16)
                for kc in range(KC):
                    mm = pe.matmul(ps_p[:, :], wqT[:, kc, pair * P:(pair + 1) * P], hq[:, kc, :],
                                   start=(kc == 0), stop=(kc == KC - 1))
                mm.then_inc(q_proj, 1)

            def score(it, c, h, pair):
                for t in range(TPC):
                    jt = c * TPC + t
                    for half in range(2):
                        mm = pe.matmul(ps_s[:, h, t, :], kst[:, pair, h, jt * P:(jt + 1) * P],
                                       qst[:, it % 2, h, half, :], start=(half == 0), stop=(half == 1))
                mm.then_inc(scores, 1)

            def broadcast(it, c):
                pe.matmul(ps_r[:, :], sel[:, c, :], rec[:, :], start=True, stop=True).then_inc(spread, 1)

            pe.wait_ge(w_saved, 3)
            for n in range(NI):
                project_k(0, n)
                pe.wait_ge(k_done, n + 1)
                project_v(0, n)
            pe.wait_ge(v_done, NI)
            project_q(0, 0)
            pe.wait_ge(q_twice, 32)
            for c in range(LEAD):
                for h in range(2):
                    if c:
                        pe.wait_ge(clipped, 2 * (c - 1) + h + 1)
                    score(0, c, h, 0)

            def body(e, b, base, it, ib, pair, first, cross, refill, more):
                g0 = it * NC
                for c in range(NC):
                    ahead = more or c + LEAD < NC
                    over = c + LEAD >= NC
                    spair = 1 - pair if over and cross else pair
                    if c == NC - LEAD and more:
                        pe.wait_ge(q_twice, it * 32 + 64)
                        if cross:
                            pe.wait_ge(k_done, it + NI + 1)
                    if ahead:
                        pe.wait_ge(clipped, g0 * 2 + 2 * (c + 1) + 1)
                        score(it + 1 if over else it, (c + LEAD) % NC, 0, spair)
                    if not first and c in RB_STEPS:
                        pe.wait_ge(rec_moved, it * 32)
                        pe.wait_ge(scaled, (it - 1) * NC + RB_STEPS[c][0])
                        broadcast(it - 1, RB_STEPS[c][0])
                    pe.wait_ge(probs, g0 * 2 + 2 * c + 2)
                    pe.wait_ge(num_saved, g0 + c)
                    if c == 0:
                        pe.wait_ge(v_done, base + NI)
                    for t in range(TPC):
                        for h in range(2):
                            mm = pe.matmul(ps_n[h * DH:(h + 1) * DH, :], vt[:, pair, c * TPC + t, h * DH:(h + 1) * DH],
                                           ex[:, c % ER, t, h, :], start=(t == 0), stop=(t == TPC - 1))
                    mm.then_inc(num_done, 1)
                    if ahead:
                        pe.wait_ge(clipped, g0 * 2 + 2 * (c + 1) + 2)
                        score(it + 1 if over else it, (c + LEAD) % NC, 1, spair)
                    if c % 2:
                        pe.wait_ge(summed, g0 + c + 1)
                        if c == 1 and not first:
                            pe.wait_ge(den_saved, it)
                        for cc in (c - 1, c):
                            for h in range(2):
                                q = (cc % 2) * 2 + h
                                mm = pe.matmul(ps_d[q * 32:(q + 1) * 32, :], onehot[:, c // 2, :],
                                               pair_sum[:, cc % ER, h, :], start=(c == 1), stop=(c == NC - 1),
                                               tile_position=(0, 32 * q))
                        mm.then_inc(den_done, 1)
                    if not first and c in RB_STEPS:
                        pe.wait_ge(scaled, (it - 1) * NC + RB_STEPS[c][1])
                        broadcast(it - 1, RB_STEPS[c][1])
                    if c == K_STEP and refill:
                        project_k(1 - pair, it + NI)
                    if c == Q_STEP and more:
                        if refill:
                            pe.wait_ge(k_done, it + NI + 1)
                        else:
                            pe.wait_ge(q_done, it + 1)
                            pe.wait_ge(v_done, NBLK)
                        project_q(1 - pair if cross else pair, it + 1)
                    if c == V_STEP and refill:
                        pe.wait_ge(q_done, it + 2)
                        project_v(1 - pair, it + NI)

            iterations(pe, body)
            for c in range(NC):
                if c == 0:
                    pe.wait_ge(rec_moved, NBLK * 32)
                pe.wait_ge(scaled, (NBLK - 1) * NC + c)
                broadcast(NBLK - 1, c)

        @block.vector
        def _(dve):
            for m, (dst, sc) in enumerate(((wqT, DH ** -0.5), (wkT, 1.0), (wvT, 1.0))):
                dve.wait_ge(w_turned, 2 * (m + 1))
                dve.tensor_scalar(dst[:, :, :], ps_s[:, 0, :, 0:F], sc, None, ALU.mult).then_inc(w_saved, 1)
            dve.wait_ge(small_in, 16 * 5)
            dve.tensor_scalar(bq[:, :], bq[:, :], DH ** -0.5, None, ALU.mult).then_inc(bias_made, 1)
            dve.tensor_copy(sel[:, :, :], sel_in[:, :, :]).then_inc(sel_made, 1)
            dve.wait_ge(bias_made, 1)

            def split_k(pair, ib, n):
                for h in range(2):
                    dve.wait_ge(k_hi, n * 2 + 2)
                    last = dve.scalar_tensor_tensor(
                        out=kst[half(1 - h), pair, h, cols(ib)], in0=ps_p[half(h), :], scalar=bk[half(h), pair:pair + 1],
                        in1=kst[half(h), pair, h, cols(ib)].bitcast(F32), op0=ALU.add, op1=ALU.subtract)
                last.then_inc(k_done, 1)

            def split_q(pair, it):
                dve.wait_ge(q_hi, it * 2 + 2)
                for h in range(2):
                    last = dve.scalar_tensor_tensor(
                        out=qst[half(h), it % 2, h, 1, :], in0=ps_p[half(h), :], scalar=bq[half(h), pair:pair + 1],
                        in1=qst[half(h), it % 2, h, 0, :].bitcast(F32), op0=ALU.add, op1=ALU.subtract)
                last.then_inc(q_done, 1)

            def copy_v(pair, ib, n):
                dve.wait_ge(v_proj, n + 1)
                dve.tensor_tensor(vt[:, pair, bass.ds(ib * TI, TI), :], ps_p[:, :].rearrange("p (t e) -> p t e", t=TI),
                                  bv[:, pair * P:(pair + 1) * P].unsqueeze(1).broadcast_to([P, TI, P]),
                                  ALU.add).then_inc(v_done, 1)

            def clip(it, c, h, ib):
                dve.wait_ge(scores, it * (2 * NC) + 2 * c + h + 1)
                dve.scalar_tensor_tensor(out=ex[:, c % ER, :, h, :], in0=ps_s[:, h, :, :], scalar=-LIM,
                                         in1=mask_log[:, c * TPC:(c + 1) * TPC, cols(ib)],
                                         op0=ALU.max, op1=ALU.min).then_inc(clipped, 1)

            def invert(it):
                dve.wait_ge(den_moved, it * 64 + 64)
                dve.reciprocal(den_t[:, :], den_t[:, :]).then_inc(inverted, 1)

            def high_rec(it):
                dve.wait_ge(inverted, it + 1)
                dve.wait_ge(rec_moved, it * 32)
                dve.tensor_copy(rec_t[:, 0, :], den_t[:, :]).then_inc(rec_hi, 1)

            def low_rec(it):
                dve.wait_ge(rec_hi, it + 1)
                dve.tensor_tensor(rec_t[:, 1, :], den_t[:, :], rec_t[:, 0, :].bitcast(F32),
                                  ALU.subtract).then_inc(rec_lo, 1)

            def scale(it, c):
                dve.wait_ge(spread, it * NC + c + 1)
                dve.wait_ge(num_saved, it * NC + c + 1)
                dve.tensor_tensor(num_slot(it, c), ps_r[:, :], num_slot(it, c), ALU.mult).then_inc(scaled, 1)

            for ib in range(NI):
                split_k(0, ib, ib)
                copy_v(0, ib, ib)
            split_q(0, 0)
            for c in range(LEAD):
                for h in range(2):
                    clip(0, c, h, 0)

            def body(e, b, base, it, ib, pair, first, cross, refill, more):
                for c in range(NC):
                    over = c + LEAD >= NC
                    if not over:
                        sit, sib = it, ib
                    else:
                        sit, sib = it + 1, 0 if cross else ib + 1
                    if more or not over:
                        if not (first and c < ER - LEAD):
                            dve.wait_ge(num_done, it * NC + c + LEAD - ER + 1)
                            dve.wait_ge(summed, it * NC + c + LEAD - ER + 1)
                        for h in range(2):
                            clip(sit, (c + LEAD) % NC, h, sib)
                            if h == 0 and not first and c == 1:
                                invert(it - 1)
                            if h == 0 and not first and c == 2:
                                low_rec(it - 1)
                            if h == 0 and not first and c in RB_STEPS:
                                scale(it - 1, RB_STEPS[c][0])
                    elif not first and c in RB_STEPS:
                        scale(it - 1, RB_STEPS[c][0])
                    if not first:
                        if c == 1:
                            high_rec(it - 1)
                        if c in RB_STEPS:
                            scale(it - 1, RB_STEPS[c][1])
                    if c == K_STEP + 1 and refill:
                        split_k(1 - pair, ib, it + NI)
                    if c == Q_STEP + 1 and more:
                        split_q(1 - pair if cross else pair, it + 1)
                    if c == V_STEP + 1 and refill:
                        copy_v(1 - pair, ib, it + NI)

            iterations(dve, body)
            last = NBLK - 1
            invert(last)
            high_rec(last)
            low_rec(last)
            for c in range(NC):
                scale(last, c)

        @block.scalar
        def _(act):
            act.wait_ge(bias_made, 1)

            def high_k(pair, ib, n):
                act.wait_ge(k_proj, n + 1)
                for h in range(2):
                    nc.scalar.activation(kst[half(h), pair, h, cols(ib)], ps_p[half(h), :], ACT.Identity,
                                         bias=bk[half(h), pair:pair + 1]).then_inc(k_hi, 1)

            def high_q(pair, it):
                act.wait_ge(q_proj, it + 1)
                for h in range(2):
                    nc.scalar.activation(qst[half(h), it % 2, h, 0, :], ps_p[half(h), :], ACT.Identity,
                                         bias=bq[half(h), pair:pair + 1]).then_inc(q_hi, 1)

            def exp(it, c, h):
                act.wait_ge(clipped, it * (2 * NC) + 2 * c + h + 1)
                e = ex[:, c % ER, :, h, :]
                nc.scalar.activation(e, e, ACT.Exp).then_inc(probs, 1)

            def save_num(it, c, first):
                act.wait_ge(num_done, it * NC + c + 1)
                if not first:
                    act.wait_ge(added, (it - 1) * (NC - 1))
                nc.scalar.copy(num_slot(it, c), ps_n[:, :]).then_inc(num_saved, 1)

            def save_den(it):
                act.wait_ge(den_done, it * (NC // 2) + NC // 2)
                act.wait_ge(den_moved, it * 64)
                nc.scalar.copy(den[:, :], ps_d[:, :]).then_inc(den_saved, 1)

            for ib in range(NI):
                high_k(0, ib, ib)
            high_q(0, 0)
            for c in range(LEAD):
                for h in range(2):
                    exp(0, c, h)

            def body(e, b, base, it, ib, pair, first, cross, refill, more):
                for c in range(NC):
                    over = c + LEAD >= NC
                    go = more or not over
                    sit = it + 1 if over else it
                    if go:
                        exp(sit, (c + LEAD) % NC, 0)
                    if c == 0 and not first:
                        save_den(it - 1)
                    save_num(it, c, first)
                    if go:
                        exp(sit, (c + LEAD) % NC, 1)
                    if c == K_STEP and refill:
                        high_k(1 - pair, ib, it + NI)
                    if c == Q_STEP and more:
                        high_q(1 - pair if cross else pair, it + 1)

            iterations(act, body)
            save_den(NBLK - 1)

        @block.gpsimd
        def _(pool):
            def pair_up(it, c, fresh=False):
                pool.wait_ge(probs, it * (2 * NC) + 2 * c + 2)
                if not fresh:
                    pool.wait_ge(den_done, it * (NC // 2) + (c - ER) // 2 + 1)
                nc.gpsimd.tensor_tensor(pair_sum[:, c % ER], ex[:, c % ER, 0], ex[:, c % ER, 1],
                                        ALU.add).then_inc(summed, 1)

            def add(it, c):
                if c == 1:
                    pool.wait_ge(scaled, it * NC + 2)
                    pool.wait_ge(ctx_out, it * 16)
                    nc.gpsimd.tensor_tensor(ctx[:, :], num_slot(it, 0), num_slot(it, 1), ALU.add).then_inc(added, 1)
                else:
                    pool.wait_ge(scaled, it * NC + c + 1)
                    pool.wait_ge(added, it * (NC - 1) + c - 1)
                    nc.gpsimd.tensor_tensor(ctx[:, :], ctx[:, :], num_slot(it, c), ALU.add).then_inc(added, 1)

            for c in range(LEAD):
                pair_up(0, c, fresh=True)

            def body(e, b, base, it, ib, pair, first, cross, refill, more):
                for c in range(NC):
                    over = c + LEAD >= NC
                    if more or not over:
                        pair_up(it + 1 if over else it, (c + LEAD) % NC, fresh=first and c < ER - LEAD)
                    if not first:
                        for cc in RB_STEPS.get(c, ()):
                            if cc:
                                add(it - 1, cc)

            iterations(pool, body)
            for c in range(1, NC):
                add(NBLK - 1, c)
    s.close()


WA = F + 2 * H


def stage_between(nc, d, ident, ecol):
    s = Scope(nc)
    NBK = B * NI
    worow = s.sb("worow", [P, KC, F])
    woT = s.sb("woT", [P, KC, F])
    waug = s.sb("waug", [P, KC, WA])
    att = s.sb("att", [P, H, 2 * DH])
    wa = s.sb("wa", [P, KC, 2, F])
    gamma, beta = s.sb("gamma", [P, F]), s.sb("beta", [P, F])
    eps = s.sb("c_eps", [P, 1])
    cT = s.sb("cT", [P, 2, KC, IB])
    hbt = s.sb("hbt", [P, 4, TI, F])
    xin = s.sb("xin", [P, 4, TI, F])
    y = s.sb("y", [P, 4, TI, F])
    x1 = s.sb("x1t", [P, 4, TI, F])
    h2 = s.sb("h2", [P, 2, TI, F])
    h2T = s.sb("h2T", [P, 2, KC, IB])
    wh = s.sb("wht", [P, 2, TI, WA])
    er = s.sb("er", [H, 2, IB])
    st = [s.sb(f"c_st{i}", [P, TI, 6]) for i in range(2)]
    mv = [s.sb(f"c_mv{i}", [P, TI, 2]) for i in range(2)]
    sd = [s.sb(f"c_sd{i}", [P, TI]) for i in range(2)]
    rs = [s.sb(f"c_rs{i}", [P, TI]) for i in range(2)]
    nb = [s.sb(f"c_nb{i}", [P, TI]) for i in range(2)]
    ps_y = s.ps("ps_y", [P, TI, F])
    ps_t = s.ps("ps_t", [P, KC, IB])
    ps_w = s.ps("ps_w", [P, 2, IB])
    ps_e = s.ps("ps_e", [H, IB])

    def sems(*names):
        return [s.sem("c_" + n) for n in names]

    w_in, wo_turned, setup, wa_made, passed = sems("w", "wot", "setup", "wa", "passed")
    c_in, hb_in, x_in = sems("cin", "hbin", "xin")
    y_proj, y_made, stat, aggr, sdd, rsd, nbd = sems("yp", "y", "stat", "aggr", "sd", "rs", "nb")
    stat2, aggr2, sdd2, rsd2, nbd2 = sems("stat2", "aggr2", "sd2", "rs2", "nb2")
    normed, scaled, xb_made, x1_made, h2_made, turned, turn_saved = sems("n", "g", "xb", "x1", "h2", "t", "ts")
    wh_proj, wh_saved, er_proj, er_saved, ec_saved = sems("whp", "whs", "erp", "ers", "ecs")
    x1_out, wh_out, er_out = sems("x1o", "who", "ero")

    def steps(e, body):
        body(0, 0, True, False, False)
        body(1, 1, True, True, False)
        for n in (2, 3):
            body(n, n % 2, True, True, True)
        with e.Fori(2, NBK // 2) as m:
            for par in range(2):
                body(m * 2 + par, par, True, True, True)
        body(NBK, 0, False, True, True)
        body(NBK + 1, 1, False, False, True)

    def nodes(ap, n):
        return ap.rearrange("b n f -> (b n) f")[bass.ds(n * IB, IB), :].rearrange("(t p) f -> p t f", p=P)

    with nc.Block() as block:

        @block.sync
        def _(sp):
            sp.dma_start(worow[:, :, :], d["wo"].rearrange("(c p) f -> p c f", p=P)).then_inc(w_in, 16)
            for kc in range(KC):
                sp.dma_start(waug[:, kc, 0:F].rearrange("p (h e) -> p h e", h=H),
                             d["w1"][:, kc * P:(kc + 1) * P, :].rearrange("h p e -> p h e")).then_inc(w_in, 16)
            for dst, src in ((att[:, :, :], d["a"]), (gamma[:, :], d["gamma"]), (beta[:, :], d["beta"])):
                sp.dma_start(dst, src.partition_broadcast(P)).then_inc(w_in, 16)

            def loads(n):
                if not isinstance(n, int):
                    pass_waits(sp, passed)
                for q in range(KC):
                    sp.dma_start(cT[:, n % 2, q, :], d["ctxT"][(n // NI) * (KC * NI) + q * NI + n % NI]).then_inc(c_in, 16)
                sp.dma_start(hbt[:, n % 4], nodes(d["hb"], n)).then_inc(hb_in, 16)
                sp.dma_start(xin[:, n % 4], nodes(d["x"], n)).then_inc(x_in, 16)

            loads(0)

            def body(n, par, s0, s1, s2):
                if s0 and not (isinstance(n, int) and n + 1 >= NBK):
                    sp.wait_ge(c_in, n * 32 + 32)
                    sp.wait_ge(hb_in, n * 16 + 16)
                    sp.wait_ge(x_in, n * 16 + 16)
                    sp.wait_ge(y_proj, n)
                    if s2:
                        pass_waits(sp, passed)
                        sp.wait_ge(x1_made, n - 2)
                    loads(n + 1)
                if s1:
                    sp.wait_ge(x1_made, n)
                    sp.wait_ge(x1_out, (n - 1) * 16)
                    pass_waits(sp, passed)
                    sp.dma_start(nodes(d["x1"], n - 1), x1[:, (n - 1) % 4]).then_inc(x1_out, 16)
                if s2:
                    sp.wait_ge(wh_saved, (n - 2) * TI + TI)
                    pass_waits(sp, passed)
                    sp.wait_ge(wh_out, (n - 2) * 16)
                    pass_waits(sp, passed)
                    sp.dma_start(wh_dst(n - 2), wh[:, par]).then_inc(wh_out, 16)
                    sp.wait_ge(er_saved, n - 1)
                    sp.wait_ge(er_out, (n - 2) * 16)
                    pass_waits(sp, passed)
                    sp.dma_start(er_dst(n - 2), er[:, par, :]).then_inc(er_out, 16)

            def wh_dst(n):
                return d["wh"][n // NI][:, bass.ds(n % NI * TI, TI), :]

            def er_dst(n):
                return d["er"][n // NI][:, bass.ds(n % NI * IB, IB)]

            body(0, 0, True, False, False)
            body(1, 1, True, True, False)
            for n in (2, 3):
                body(n, n % 2, True, True, True)
            with sp.Fori(2, NBK // 2 - 1) as m:
                for par in range(2):
                    body(m * 2 + par, par, True, True, True)
            for n in (NBK - 2, NBK - 1):
                body(n, n % 2, True, True, True)
            body(NBK, 0, False, True, True)
            body(NBK + 1, 1, False, False, True)
            sp.wait_ge(x1_out, 16 * NBK)
            sp.wait_ge(wh_out, 16 * NBK)
            sp.wait_ge(er_out, 16 * NBK)

        @block.tensor
        def _(pe):
            pe.wait_ge(w_in, 16 * 6)
            for kc in range(KC):
                for oc in range(KC):
                    mm = pe.transpose(ps_t[:, kc, oc * P:(oc + 1) * P], worow[:, oc, kc * P:(kc + 1) * P], ident[:, :])
            mm.then_inc(wo_turned, 1)
            pe.wait_ge(setup, 2)
            pe.wait_ge(wa_made, 4)

            def body(n, par, s0, s1, s2):
                if s2:
                    pe.wait_ge(h2_made, (n - 1) * TI)
                    if not isinstance(n, int) or n > 2:
                        pe.wait_ge(turn_saved, (n - 2) * KC)
                    for kc in range(KC):
                        for t in range(TI):
                            mm = pe.transpose(ps_t[:, kc, t * P:(t + 1) * P], h2[:, par, t, kc * P:(kc + 1) * P],
                                              ident[:, :])
                        mm.then_inc(turned, 1)
                if s0:
                    pe.wait_ge(c_in, n * 32 + 32)
                    pe.wait_ge(y_made, n)
                    for t in range(TI):
                        for kc in range(KC):
                            mm = pe.matmul(ps_y[:, t, :], cT[:, par, kc, t * P:(t + 1) * P], woT[:, kc, :],
                                           start=(kc == 0), stop=(kc == KC - 1))
                    mm.then_inc(y_proj, 1)
                if s2:
                    pe.wait_ge(turn_saved, (n - 1) * KC)
                    pe.wait_ge(er_saved, n - 2)
                    for kc in range(KC):
                        mm = pe.matmul(ps_e[:, :], waug[:, kc, F:F + H], h2T[:, par, kc, :],
                                       start=(kc == 0), stop=(kc == KC - 1))
                    mm.then_inc(er_proj, 1)
                    for t in range(TI):
                        pe.wait_ge(wh_saved, (n - 2) * TI + max(t - 1, 0))
                        for kc in range(KC):
                            mm = pe.matmul(ps_w[:, t % 2, 0:WA], h2T[:, par, kc, t * P:(t + 1) * P], waug[:, kc, :],
                                           start=(kc == 0), stop=(kc == KC - 1))
                        mm.then_inc(wh_proj, 1)

            steps(pe, body)

        @block.vector
        def _(dve):
            dve.memset(eps[:, :], EPS).then_inc(setup, 1)
            dve.wait_ge(wo_turned, 1)
            dve.tensor_copy(woT[:, :, :], ps_t[:, :, 0:F]).then_inc(setup, 1)
            dve.wait_ge(w_in, 16 * 6)
            for j in range(2):
                for kc in range(KC):
                    dve.tensor_tensor(wa[:, kc, j, :].rearrange("p (h e) -> p h e", h=H),
                                      waug[:, kc, 0:F].rearrange("p (h e) -> p h e", h=H),
                                      att[:, :, j * DH:(j + 1) * DH], ALU.mult).then_inc(wa_made, 1)
            dve.wait_ge(wa_made, 4)
            for j in range(2):
                for kc in range(KC):
                    dve.tensor_reduce(waug[:, kc, F + j * H:F + (j + 1) * H],
                                      wa[:, kc, j, :].rearrange("p (h e) -> p h e", h=H), AX.X,
                                      ALU.add).then_inc(wa_made, 1)

            def statistics(i, src, n, ss, sa, readers):
                for sem, v in readers:
                    dve.wait_ge(sem, v)
                pass_waits(dve, passed)
                for t in range(TI):
                    dve.bn_stats(st[i][:, t, :], src[:, t, :]).then_inc(ss, 1)
                dve.wait_ge(ss, n * TI + TI)
                pass_waits(dve, passed)
                for t in range(TI):
                    dve.bn_aggr(mv[i][:, t, :], st[i][:, t, :]).then_inc(sa, 1)

            def invert(i, n, s_sd, s_rs, s_nb, s_read, per):
                dve.wait_ge(s_sd, n + 1)
                dve.wait_ge(s_read, n * per)
                dve.reciprocal(rs[i][:, :], sd[i][:, :]).then_inc(s_rs, 1)
                dve.wait_ge(s_rs, n + 1)
                dve.scalar_tensor_tensor(out=nb[i][:, :], in0=mv[i][:, :, 0], scalar=-1.0, in1=rs[i][:, :],
                                         op0=ALU.mult, op1=ALU.mult).then_inc(s_nb, 1)

            def body(n, par, s0, s1, s2):
                if s0:
                    dve.wait_ge(y_proj, n + 1)
                    dve.wait_ge(hb_in, n * 16 + 16)
                    if s2:
                        dve.wait_ge(x1_made, n - 2)
                    dve.tensor_tensor(y[:, n % 4], ps_y[:, :, :], hbt[:, n % 4], ALU.add).then_inc(y_made, 1)
                    dve.wait_ge(y_made, n + 1)
                    statistics(0, y[:, n % 4], n, stat, aggr, ((aggr, n * TI), (nbd, n), (sdd, n)))
                if s1:
                    p = n - 1
                    dve.wait_ge(scaled, n)
                    dve.wait_ge(xb_made, n)
                    if not isinstance(n, int) or n > 4:
                        dve.wait_ge(x1_out, (n - 4) * 16)
                    dve.tensor_tensor(x1[:, p % 4], y[:, p % 4], xin[:, p % 4], ALU.add).then_inc(x1_made, 1)
                    dve.wait_ge(x1_made, n)
                    statistics(1, x1[:, p % 4], p, stat2, aggr2, ((aggr2, p * TI), (nbd2, p), (sdd2, p)))
                if s0:
                    invert(0, n, sdd, rsd, nbd, normed, TI)
                if s1:
                    invert(1, n - 1, sdd2, rsd2, nbd2, h2_made, TI)
                if s2:
                    q = n - 2
                    if not isinstance(n, int) or n > 3:
                        dve.wait_ge(wh_out, (n - 3) * 16)
                        dve.wait_ge(ec_saved, n - 3)
                    for t in range(TI):
                        dve.wait_ge(wh_proj, q * TI + t + 1)
                        dve.tensor_copy(wh[:, par, t, :], ps_w[:, t % 2, 0:WA]).then_inc(wh_saved, 1)

            steps(dve, body)

        @block.scalar
        def _(act):
            act.wait_ge(setup, 2)

            def root(i, n, s_aggr, s_sd, s_rs):
                act.wait_ge(s_aggr, n * TI + TI)
                act.wait_ge(s_rs, n)
                nc.scalar.activation(sd[i][:, :], mv[i][:, :, 1], ACT.Sqrt, bias=eps[:, 0:1]).then_inc(s_sd, 1)

            def body(n, par, s0, s1, s2):
                if s0:
                    root(0, n, aggr, sdd, rsd)
                if s2:
                    for kc in range(KC):
                        act.wait_ge(turned, (n - 2) * KC + kc + 1)
                        nc.scalar.copy(h2T[:, par, kc, :], ps_t[:, kc, :]).then_inc(turn_saved, 1)
                if s1:
                    root(1, n - 1, aggr2, sdd2, rsd2)
                if s0:
                    act.wait_ge(nbd, n + 1)
                    for t in range(TI):
                        nc.scalar.activation(y[:, n % 4, t, :], y[:, n % 4, t, :], ACT.Identity, bias=nb[0][:, t:t + 1],
                                             scale=rs[0][:, t:t + 1]).then_inc(normed, 1)
                if s1:
                    p = n - 1
                    act.wait_ge(nbd2, n)
                    if s2:
                        act.wait_ge(turned, (n - 2) * KC)
                    for t in range(TI):
                        nc.scalar.activation(h2[:, 1 - par, t, :], x1[:, p % 4, t, :], ACT.Relu,
                                             bias=nb[1][:, t:t + 1], scale=rs[1][:, t:t + 1]).then_inc(h2_made, 1)
                if s2:
                    act.wait_ge(er_proj, n - 1)
                    if not isinstance(n, int) or n > 3:
                        act.wait_ge(er_out, (n - 3) * 16)
                    nc.scalar.copy(er[:, par, :], ps_e[:, :]).then_inc(er_saved, 1)

            steps(act, body)

        @block.gpsimd
        def _(pool):
            pool.wait_ge(w_in, 16 * 6)

            def row(ap):
                return ap[:, :].unsqueeze(1).broadcast_to([P, TI, F])

            def body(n, par, s0, s1, s2):
                if s0:
                    pool.wait_ge(x_in, n * 16 + 16)
                    nc.gpsimd.tensor_tensor(xin[:, n % 4], xin[:, n % 4], row(beta), ALU.add).then_inc(xb_made, 1)
                    pool.wait_ge(normed, n * TI + TI)
                    nc.gpsimd.tensor_tensor(y[:, n % 4], y[:, n % 4], row(gamma), ALU.mult).then_inc(scaled, 1)
                if s2:
                    pool.wait_ge(wh_saved, (n - 1) * TI)
                    nc.gpsimd.tensor_copy(ecol[:, bass.ds((n - 2) * TI, TI), :],
                                          wh[:, par, :, F + H:WA]).then_inc(ec_saved, 1)

            steps(pool, body)
    s.close()


QB = 2 * IB
QT = QB // P
NQ = N // QB
NP8 = NT // NQ
NEG = 1.0 - ALPHA


def stage_graph(nc, d, ident, ecol):
    s = Scope(nc)
    NIT = B * NQ
    m01 = s.sb("m01", [P, NT, N], I8)
    gmax = s.sb("gmax", [P, B * H])
    gall = s.sb("gall", [P, B * H])
    tau = s.sb("tau", [P, B * NT, H])
    vp = s.sb("vp", [P, B * NT, H])
    whin = s.sb("whin", [P, NP8, WA])
    tree = s.sb("tree", [P, 4, F])
    whsum = s.sb("whsum", [P, 4, F])
    whred = s.sb("whred", [P, F])
    whall = s.sb("whall", [P, F])
    vq = s.sb("vq", [P, 2, NT, H, DH])
    vrep = s.sb("vrep", [P, 2, NT, H, 32])
    rho = s.sb("rho", [P, 2, H, QB])
    pr = s.sb("pr", [P, 2, H, QB])
    ns = s.sb("ns", [P, KC, QB])
    ds = s.sb("ds", [P, QB])
    u = s.sb("u", [P, QT, F])
    den = s.sb("den", [P, QT, H])
    empty = s.sb("empty", [P, QT, H])
    dz = s.sb("dz", [P, QT, H])
    rinv = s.sb("rinv", [P, QT, H])
    eb = s.sb("eb", [P, QT, F])
    xo = s.sb("xo", [P, QT, F])
    ps_n = s.ps("ps_n2", [P, KC, QB])
    ps_d = s.ps("ps_d2", [P, QB])
    ps_t = s.ps("ps_t2", [P, 2, IB])

    def sems(*names):
        return [s.sem("d_" + n) for n in names]

    m_in, wh_in, er_in, x1_in, stored = sems("m", "whin", "er", "x1", "st")
    gm, gr, ed, terms, passed = sems("gm", "gr", "ed", "terms", "passed")
    vq_made, vrep_made, sum_made, treed, wh_read = sems("vq", "vrep", "sum", "tree", "whr")
    rho_relu, rho_made, pr_made, used = sems("rrelu", "rho", "pr", "used")
    n_done = sems("nd0", "nd1")
    n_saved = sems("ns0", "ns1")
    d_saved, turned, raw = sems("ds", "turn", "raw")
    flagged, inverted, pool_step, mixed, low, expd, elu, out_made = sems(
        "flag", "inv", "ps", "mix", "low", "exp", "elu", "out")

    def iterations(e, body):
        body(0, 0, 0, 0, False)
        body(1, 0, 1, 0, True)

        def batch(b, par):
            with e.Fori(0, NQ) as blk:
                body(b * NQ + blk, b, blk, par, True)
        batch(1, 1)
        with e.Fori(1, B // 2) as bb:
            batch(bb * 2, 0)
            batch(bb * 2 + 1, 1)

    def half(ap):
        return ap.rearrange("(t p) f -> p t f", p=P)

    with nc.Block() as block:

        @block.sync
        def _(sp):
            def load_wh(n):
                if not isinstance(n, int):
                    pass_waits(sp, passed)
                sp.dma_start(whin[:, :, :], d["wh"][n // 2][:, bass.ds(n % 2 * NP8, NP8), :]).then_inc(wh_in, 16)

            def load_er(t, slot):
                if not isinstance(t, int):
                    pass_waits(sp, passed)
                sp.dma_start(rho[:, slot], d["er"][t // NQ][:, bass.ds(t % NQ * QB, QB)].partition_broadcast(P)).then_inc(
                    er_in, 16)

            def node_rows(ap, t):
                return half(ap[t // NQ][bass.ds(t % NQ * QB, QB), :])

            load_er(0, 0)
            load_wh(0)
            sp.dma_start(m01[:, :, :], d["mask01"]).then_inc(m_in, 16)
            sp.wait_ge(wh_read, 1)
            load_wh(1)
            sp.wait_ge(er_in, 16)

            def epilogue(t):
                sp.wait_ge(out_made, t)
                pass_waits(sp, passed)
                sp.dma_start(xo[:, :, :], node_rows(d["x1"], t)).then_inc(x1_in, 16)
                sp.wait_ge(out_made, t + 1)
                pass_waits(sp, passed)
                sp.dma_start(node_rows(d["out"], t), eb[:, :, :]).then_inc(stored, 16)

            def body(t, b, blk, par, before):
                if before:
                    sp.wait_ge(used, t * NT)
                load_er((t + 1) % NIT, (t + 1) % 2)
                sp.wait_ge(wh_read, t + 2)
                load_wh((t + 2) % NIT)
                if before:
                    epilogue(t - 1)
                sp.wait_ge(er_in, t * 16 + 32)
                pass_waits(sp, passed)

            iterations(sp, body)
            epilogue(NIT - 1)
            sp.wait_ge(stored, 16 * NIT)
            sp.wait_ge(wh_in, 16 * (NIT + 2))

        @block.tensor
        def _(pe):
            pe.wait_ge(terms, 2)

            def turn(t, k):
                pe.wait_ge(n_saved[0], t + 1)
                pe.wait_ge(n_saved[1], t + 1)
                pe.wait_ge(d_saved, t + 1)
                if k >= 2:
                    pe.wait_ge(raw, t * QT + k - 1)
                else:
                    pe.wait_ge(raw, t * QT)
                for j, src in enumerate((ns[:, 0], ns[:, 1], ds)):
                    mm = pe.transpose(ps_t[:, k % 2, j * P:(j + 1) * P], src[:, k * P:(k + 1) * P], ident[:, :])
                mm.then_inc(turned, 1)

            def body(t, b, blk, par, before):
                pe.wait_ge(vq_made, b * 2 + 2)
                pe.wait_ge(vrep_made, b * 2 + 2)
                for jt in range(NT):
                    first, last = jt == 0, jt == NT - 1
                    for p in range(KC):
                        pe.wait_ge(pr_made, t * (NT * H) + jt * H + 2 * p + 2)
                        if first:
                            pe.wait_ge(n_saved[p], t)
                        for ih in range(2):
                            for hh in range(2):
                                mm = pe.matmul(ps_n[hh * DH:(hh + 1) * DH, p, ih * IB:(ih + 1) * IB],
                                               vq[:, par, jt, 2 * p + hh, :],
                                               pr[:, jt % 2, 2 * p + hh, ih * IB:(ih + 1) * IB], start=first, stop=last)
                        if last:
                            mm.then_inc(n_done[p], 1)
                    if first:
                        pe.wait_ge(d_saved, t)
                    for ih in range(2):
                        for h in range(H):
                            mm = pe.matmul(ps_d[h * 32:(h + 1) * 32, ih * IB:(ih + 1) * IB], vrep[:, par, jt, h, :],
                                           pr[:, jt % 2, h, ih * IB:(ih + 1) * IB], start=first, stop=last,
                                           tile_position=(0, 32 * h))
                    mm.then_inc(used, 1)
                    if before and 2 <= jt < 2 + QT:
                        turn(t - 1, jt - 2)

            iterations(pe, body)
            for k in range(QT):
                turn(NIT - 1, k)

        @block.vector
        def _(dve):
            dve.tensor_reduce(gmax[:, :].rearrange("p (b h) -> p b h", h=H),
                              ecol[:, :, :].rearrange("p (b t) h -> p b h t", t=NT), AX.X, ALU.max).then_inc(gm, 1)
            dve.wait_ge(gr, 1)
            dve.tensor_tensor(ecol[:, :, :].rearrange("p (b t) h -> p b t h", t=NT),
                              ecol[:, :, :].rearrange("p (b t) h -> p b t h", t=NT),
                              gall[:, :].rearrange("p (b h) -> p b h", h=H).unsqueeze(2).broadcast_to([P, B, NT, H]),
                              ALU.subtract).then_inc(ed, 1)
            dve.wait_ge(terms, 2)
            dve.wait_ge(m_in, 16)

            def finish_a(t):
                dve.wait_ge(raw, (t + 1) * QT)
                dve.wait_ge(mixed, t)
                dve.tensor_scalar(empty[:, :, :], den[:, :, :], 0.0, None, ALU.is_equal).then_inc(flagged, 1)
                dve.wait_ge(flagged, t * 2 + 1)
                dve.scalar_tensor_tensor(out=dz[:, :, :], in0=empty[:, :, :], scalar=float(N), in1=den[:, :, :],
                                         op0=ALU.mult, op1=ALU.add).then_inc(flagged, 1)
                dve.wait_ge(flagged, t * 2 + 2)
                dve.reciprocal(rinv[:, :, :], dz[:, :, :]).then_inc(inverted, 1)

            def finish_b(t):
                dve.wait_ge(mixed, t + 1)
                dve.tensor_scalar(eb[:, :, :], u[:, :, :], 0.0, None, ALU.min).then_inc(low, 1)

            def finish_c(t):
                dve.wait_ge(expd, t + 1)
                dve.scalar_tensor_tensor(out=eb[:, :, :], in0=u[:, :, :], scalar=0.0, in1=eb[:, :, :],
                                         op0=ALU.max, op1=ALU.add).then_inc(elu, 1)
                dve.wait_ge(elu, t + 1)
                dve.wait_ge(x1_in, t * 16 + 16)
                dve.scalar_tensor_tensor(out=eb[:, :, :], in0=eb[:, :, :], scalar=-1.0, in1=xo[:, :, :],
                                         op0=ALU.add, op1=ALU.add).then_inc(out_made, 1)

            def body(t, b, blk, par, before):
                dve.wait_ge(rho_made, t + 1)
                for jt in range(NT):
                    if before or jt >= 2:
                        dve.wait_ge(used, t * NT + jt - 1)
                    for h in range(H):
                        dve.scalar_tensor_tensor(out=pr[:, jt % 2, h, :], in0=rho[:, t % 2, h, :],
                                                 scalar=tau[:, b * NT + jt, h:h + 1],
                                                 in1=m01[:, jt, bass.ds(blk * QB, QB)], op0=ALU.max,
                                                 op1=ALU.mult).then_inc(pr_made, 1)
                    if before:
                        if jt == 10:
                            finish_a(t - 1)
                        if jt == 13:
                            finish_b(t - 1)
                        if jt == 14:
                            finish_c(t - 1)

            iterations(dve, body)
            finish_a(NIT - 1)
            finish_b(NIT - 1)
            finish_c(NIT - 1)

        @block.scalar
        def _(act):
            act.wait_ge(ed, 1)
            nc.scalar.activation(tau[:, :, :], ecol[:, :, :], ACT.Exp, scale=NEG).then_inc(terms, 1)
            nc.scalar.activation(vp[:, :, :], ecol[:, :, :], ACT.Exp, scale=ALPHA).then_inc(terms, 1)
            act.wait_ge(terms, 2)

            def replicate(n, par):
                b, hf = n // 2, n % 2
                nc.scalar.copy(vrep[:, par, bass.ds(hf * NP8, NP8), :, :],
                               vp[:, bass.ds(n * NP8, NP8), :].unsqueeze(3).broadcast_to([P, NP8, H, 32])).then_inc(
                                   vrep_made, 1)

            def make_rho(t, n):
                act.wait_ge(er_in, t * 16 + 16)
                for h in range(H):
                    nc.scalar.activation(rho[:, t % 2, h, :], rho[:, t % 2, h, :], ACT.Relu,
                                         bias=gall[:, bass.ds(n // NQ * H + h, 1)]).then_inc(rho_relu, 1)
                act.wait_ge(rho_relu, t * H + H)
                pass_waits(act, passed)
                nc.scalar.activation(rho[:, t % 2], rho[:, t % 2], ACT.Exp, scale=-NEG).then_inc(rho_made, 1)

            def save(t):
                act.wait_ge(turned, t * QT)
                for p in range(KC):
                    act.wait_ge(n_done[p], t + 1)
                    nc.scalar.copy(ns[:, p, :], ps_n[:, p, :]).then_inc(n_saved[p], 1)
                act.wait_ge(used, (t + 1) * NT)
                nc.scalar.copy(ds[:, :], ps_d[:, :]).then_inc(d_saved, 1)

            def take(t):
                act.wait_ge(out_made, t)
                act.wait_ge(inverted, t)
                for k in range(QT):
                    act.wait_ge(turned, t * QT + k + 1)
                    nc.scalar.copy(u[:, k, :], ps_t[:, k % 2, 0:F])
                    nc.scalar.copy(den[:, k, :], ps_t[:, k % 2, F:F + P].rearrange("p (h r) -> p h r", h=H)[:, :, 0]
                                   ).then_inc(raw, 1)

            def exponent(t):
                act.wait_ge(low, t + 1)
                nc.scalar.activation(eb[:, :, :], eb[:, :, :], ACT.Exp).then_inc(expd, 1)

            replicate(0, 0)
            replicate(1, 0)
            make_rho(0, 0)

            def body(t, b, blk, par, before):
                if before:
                    save(t - 1)
                    act.wait_ge(used, (t - 1) * NT)
                replicate((t + 2) % NIT, 1 - par)
                if before:
                    take(t - 1)
                make_rho(t + 1, (t + 1) % NIT)
                if before:
                    exponent(t - 1)

            iterations(act, body)
            save(NIT - 1)
            take(NIT - 1)
            exponent(NIT - 1)

        @block.gpsimd
        def _(pool):
            pool.wait_ge(gm, 1)
            nc.gpsimd.partition_all_reduce(gall[:, :], gmax[:, :], P, bass.bass_isa.ReduceOp.max).then_inc(gr, 1)
            pool.wait_ge(terms, 2)

            def values(k, n, par):
                hf = n % 2
                pool.wait_ge(wh_in, k * 16 + 16)
                nc.gpsimd.tensor_tensor(vq[:, par, bass.ds(hf * NP8, NP8), :, :],
                                        whin[:, :, 0:F].rearrange("p t (h e) -> p t h e", h=H),
                                        vp[:, bass.ds(n * NP8, NP8), :].unsqueeze(3).broadcast_to([P, NP8, H, DH]),
                                        ALU.mult).then_inc(vq_made, 1)
                w = NP8 // 2
                nc.gpsimd.tensor_tensor(tree[:, :, :], whin[:, 0:w, 0:F], whin[:, w:NP8, 0:F], ALU.add).then_inc(wh_read, 1)
                pool.wait_ge(wh_read, k + 1)
                nc.gpsimd.tensor_tensor(tree[:, 0:2, :], tree[:, 0:2, :], tree[:, 2:4, :], ALU.add).then_inc(treed, 1)
                pool.wait_ge(treed, 3 * k + 1)
                nc.gpsimd.tensor_tensor(tree[:, 0, :], tree[:, 0, :], tree[:, 1, :], ALU.add).then_inc(treed, 1)
                pool.wait_ge(treed, 3 * k + 2)
                pass_waits(pool, passed)
                nc.gpsimd.partition_all_reduce(whred[:, :], tree[:, 0, :], P,
                                               bass.bass_isa.ReduceOp.add).then_inc(treed, 1)
                pool.wait_ge(treed, 3 * k + 3)
                nc.gpsimd.tensor_copy(whsum[:, n % 4, :], whred[:, :]).then_inc(sum_made, 1)
                pool.wait_ge(sum_made, k + 1)

            def mix(t):
                pool.wait_ge(inverted, t + 1)
                pool.wait_ge(stored, t * 16)
                nc.gpsimd.tensor_tensor(whall[:, :], whsum[:, t // NQ % 2 * 2, :], whsum[:, t // NQ % 2 * 2 + 1, :],
                                        ALU.add).then_inc(pool_step, 1)
                pool.wait_ge(pool_step, t * 3 + 1)

                def per_head(ap):
                    return ap[:, :, :].unsqueeze(3).broadcast_to([P, QT, H, DH])

                def split(ap):
                    return ap[:, :, :].rearrange("p t (h e) -> p t h e", h=H)

                nc.gpsimd.tensor_tensor(split(eb), whall[:, :].rearrange("p (h e) -> p h e", h=H).unsqueeze(1)
                                        .broadcast_to([P, QT, H, DH]), per_head(empty), ALU.mult).then_inc(pool_step, 1)
                pool.wait_ge(pool_step, t * 3 + 2)
                nc.gpsimd.tensor_tensor(u[:, :, :], u[:, :, :], eb[:, :, :], ALU.add).then_inc(pool_step, 1)
                pool.wait_ge(pool_step, t * 3 + 3)
                nc.gpsimd.tensor_tensor(split(u), split(u), per_head(rinv), ALU.mult).then_inc(mixed, 1)

            values(0, 0, 0)
            values(1, 1, 0)

            def body(t, b, blk, par, before):
                if before:
                    pool.wait_ge(used, (t - 1) * NT)
                if before:
                    mix(t - 1)
                values(t + 2, (t + 2) % NIT, 1 - par)

            iterations(pool, body)
            mix(NIT - 1)
    s.close()


def build(nc, ins, out):
    def scratch(name, shape, dt=F32):
        return nc.dram_tensor(name, shape, dt).ap()

    keep = Scope(nc)
    ident = keep.sb("ident", [P, P])
    ecol = keep.sb("ecol", [P, B * NT, H])
    d = dict(
        ins, out=out,
        hT=scratch("s_hT", (B, P, KC, N)), hb=scratch("s_hb", (B, N, F)),
        mask01=scratch("s_mask01", (P, NT, N), I8),
        ctxT=scratch("s_ctxT", (B * KC * NI, P, IB)), x1=scratch("s_x1", (B, N, F)),
        wh=scratch("s_wh", (B, P, NT, WA)), er=scratch("s_er", (B, H, N)))
    layer0 = Scope(nc)
    mask_log = layer0.sb("mask_log", [P, NT, N], I8)
    stage_prepare(nc, d, ident, mask_log)
    stage_attend(nc, d, ident, mask_log)
    layer0.close()
    stage_between(nc, d, ident, ecol)
    stage_graph(nc, d, ident, ecol)
    keep.close()


_INS = {"x": "x", "adj": "adj", "L0_gnn_Wq": "wq", "L0_gnn_bq": "bq", "L0_gnn_Wk": "wk", "L0_gnn_bk": "bk",
        "L0_gnn_Wv": "wv", "L0_gnn_bv": "bv", "L0_gnn_Wo": "wo", "L0_gnn_bo": "bo", "L0_gnn_gamma": "gamma",
        "L0_gnn_beta": "beta", "L1_gnn_W": "w1", "L1_gnn_a": "a"}


def constants():
    import numpy as np

    onehot = np.zeros((P, NC // 2, 32), np.float32)
    sel = np.zeros((4 * NC, NC, P), np.float32)
    for m in range(32):
        onehot[:, m % 4, m] = 1.0
    for half in range(2):
        for c in range(NC):
            for h in range(2):
                row = half * 2 * NC + ((c % 2) * 2 + h) * (NC // 2) + c // 2
                sel[row, c, h * DH:(h + 1) * DH] = 1.0
    return {"ident": np.eye(P, dtype=np.float32), "onehot": onehot, "sel": sel}


def kernel(**inputs):
    import numpy as np
    import concourse.bacc as bacc
    from concourse.bass_utils import run_bass_kernel_spmd as run

    nc = bacc.Bacc("TRN2", target_bir_lowering=False, num_devices=1)
    arrays, ins = {}, {}
    for name, a in [(k, np.ascontiguousarray(inputs[i])) for i, k in _INS.items()] + list(constants().items()):
        arrays[f"in_{name}"] = a
        ins[name] = nc.dram_tensor(f"in_{name}", a.shape, mybir.dt.from_np(a.dtype), kind="ExternalInput").ap()
    out = nc.dram_tensor("out_0", (B, N, F), F32, kind="ExternalOutput").ap()
    build(nc, ins, out)
    r = run(nc, [arrays], core_ids=[0])
    return r.results[0]["out_0"]
```

```python
from contextlib import ExitStack

import concourse.bass as bass
from concourse import mybir

F32 = mybir.dt.float32
F32R = mybir.dt.float32r
BF16 = mybir.dt.bfloat16
I8 = mybir.dt.int8
I32 = mybir.dt.int32
ALU = mybir.AluOpType
ACT = mybir.ActivationFunctionType
AX = mybir.AxisListType

P = 128
B, N, F = 8, 2048, 256
H, DH = 4, 64
KC = F // P
NT = N // P
IB = 512
NI = N // IB
TI = IB // P
CH = 256
NC = N // CH
LIM = 10.0
EPS = 1e-5
ALPHA = 0.2


def pass_waits(e, sem):
    e.sem_inc(sem, 1)


class Scope:

    def __init__(self, nc):
        self.nc, self.stack = nc, ExitStack()

    def sb(self, name, shape, dt=F32):
        return self.stack.enter_context(self.nc.sbuf_tensor(name, shape, dt))

    def ps(self, name, shape, dt=F32):
        return self.stack.enter_context(self.nc.psum_tensor(name, shape, dt))

    def sem(self, name):
        return self.stack.enter_context(self.nc.semaphore(name))

    def close(self):
        self.stack.close()


def stage_prepare(nc, d, ident, mask_log, hnorm):
    s = Scope(nc)
    identb = s.sb("identb", [P, P], BF16)
    eps = s.sb("a_eps", [P, 1])
    minus20 = s.sb("minus20", [P, 1])
    xt = s.sb("xt", [P, 2, NT, F])
    hs = s.sb("hs", [P, NT, F])
    hT = s.sb("hT", [P, KC, N])
    stats = s.sb("stats", [P, NT, 6])
    mv = s.sb("mv", [P, NT, 2])
    sd = s.sb("sd", [P, NT])
    rs = s.sb("rs", [P, NT])
    nb = s.sb("nb", [P, NT])
    adjt = s.sb("adjt", [P, 2, 2, N], I32)
    edge20 = s.sb("edge20", [P, N], BF16)
    code = s.sb("code", [P, 2, N], BF16)
    mask01 = s.sb("mask01", [P, NT, N], I8)
    ps_h = s.ps("ps_h", [P, KC, IB])
    HALF = NT // 2
    ps_m = s.ps("ps_m", [P, 2, 2, HALF, P], BF16)

    consts, xload, passed = s.sem("a_consts"), s.sem("a_x"), s.sem("a_passed")
    adj_in = (s.sem("a_adj0"), s.sem("a_adj1"))
    setup, statd, aggrd, sdd, rsd, nbd = (s.sem("a_" + n) for n in ("setup", "stat", "aggr", "sd", "rs", "nb"))
    h_made, norm_kept, h_turned, h_saved = (s.sem("a_" + n) for n in ("h", "keep", "hturn", "hsave"))
    hT_out, m_out = (s.sem("a_" + n) for n in ("hTo", "mo"))
    edged, coded, m_turned, log_made, m01_made = (s.sem("a_" + n) for n in ("edge", "code", "mt", "log", "m01"))

    def itile(b, k):
        return bass.ds((b * 2 + k) * P, P)

    with nc.Block() as block:

        @block.sync
        def _(sp):
            def load_adj(b):
                for k in range(2):
                    sp.dma_start(adjt[:, b % 2, k, :], d["adj"][itile(b, k), :]).then_inc(adj_in[k], 16)

            def load_x(b):
                if not isinstance(b, int):
                    pass_waits(sp, passed)
                sp.dma_start(xt[:, b % 2], d["x"][b].rearrange("(t p) f -> p t f", p=P)).then_inc(xload, 16)

            def store(b):
                sp.wait_ge(h_saved, b * (2 * NI) + 2 * NI)
                pass_waits(sp, passed)
                sp.dma_start(d["hT"][b], hT[:, :, :]).then_inc(hT_out, 16)

            load_x(0)
            sp.dma_start(ident[:, :], d["ident"]).then_inc(consts, 16)
            load_adj(0)
            sp.wait_ge(xload, 16)
            load_x(1)
            for k in range(2):
                sp.wait_ge(adj_in[k], 16)
            load_adj(1)
            with sp.Fori(0, B - 2) as b:
                sp.wait_ge(coded, b * 2 + 2)
                for k in range(2):
                    sp.wait_ge(adj_in[k], b * 16 + 32)
                load_adj(b + 2)
                sp.wait_ge(h_made, b * NT + NT)
                pass_waits(sp, passed)
                sp.wait_ge(xload, b * 16 + 32)
                load_x(b + 2)
                store(b)
            last = 2 * P * (B - 2)
            sp.wait_ge(m01_made, 4 * (B - 2))
            sp.dma_start(d["mask01"][:, :, 0:last], mask01[:, :, 0:last]).then_inc(m_out, 16)
            store(B - 2)
            store(B - 1)
            sp.wait_ge(m01_made, 4 * B)
            sp.dma_start(d["mask01"][:, :, last:N], mask01[:, :, last:N]).then_inc(m_out, 16)
            sp.wait_ge(m_out, 32)
            sp.wait_ge(hT_out, 16 * B)

        @block.vector
        def _(dve):
            dve.memset(eps[:, :], EPS).then_inc(setup, 1)
            dve.memset(minus20[:, :], -20.0).then_inc(setup, 1)
            dve.wait_ge(consts, 16)
            dve.tensor_copy(identb[:, :], ident[:, :]).then_inc(setup, 1)
            def encode(b, k):
                dve.wait_ge(adj_in[k], b * 16 + 16)
                dve.wait_ge(coded, b * 2 + k)
                dve.tensor_scalar(edge20[:, :], adjt[:, b % 2, k, :], 0, 20.0, ALU.not_equal,
                                  ALU.mult).then_inc(edged, 1)
                dve.wait_ge(edged, b * 2 + k + 1)
                dve.wait_ge(m_turned, b * 4)
                dve.scalar_tensor_tensor(out=code[:, k, :], in0=adjt[:, b % 2, k, :], scalar=0, in1=edge20[:, :],
                                         op0=ALU.is_gt, op1=ALU.add).then_inc(coded, 1)

            with dve.Fori(0, B) as b:
                dve.wait_ge(xload, b * 16 + 16)
                dve.wait_ge(aggrd, b * NT)
                pass_waits(dve, passed)
                for t in range(NT):
                    dve.bn_stats(stats[:, t, :], xt[:, b % 2, t, :]).then_inc(statd, 1)
                dve.wait_ge(statd, b * NT + NT)
                dve.wait_ge(nbd, b)
                dve.wait_ge(sdd, b)
                pass_waits(dve, passed)
                for t in range(NT):
                    dve.bn_aggr(mv[:, t, :], stats[:, t, :]).then_inc(aggrd, 1)
                encode(b, 0)
                dve.wait_ge(sdd, b + 1)
                dve.wait_ge(h_made, b * NT)
                dve.wait_ge(norm_kept, b * 2)
                dve.reciprocal(rs[:, :], sd[:, :]).then_inc(rsd, 1)
                dve.wait_ge(rsd, b + 1)
                dve.scalar_tensor_tensor(out=nb[:, :], in0=mv[:, :, 0], scalar=-1.0, in1=rs[:, :],
                                         op0=ALU.mult, op1=ALU.mult).then_inc(nbd, 1)
                encode(b, 1)
                for k in range(2):
                    for half in range(2):
                        dve.wait_ge(m_turned, b * 4 + 2 * k + half + 1)
                        dve.tensor_scalar(mask_log[:, half * HALF:(half + 1) * HALF, itile(b, k)], ps_m[:, k, half],
                                          20.0, -LIM, ALU.min, ALU.add).then_inc(log_made, 1)

        @block.scalar
        def _(act):
            act.wait_ge(setup, 3)

            def layer1_mask(b, k):
                for half in range(2):
                    act.wait_ge(log_made, b * 4 + 2 * k + half + 1)
                    nc.scalar.activation(mask01[:, half * HALF:(half + 1) * HALF, itile(b, k)], ps_m[:, k, half],
                                         ACT.Relu, bias=minus20[:, 0:1]).then_inc(m01_made, 1)

            with act.Fori(0, B) as b:
                act.wait_ge(aggrd, b * NT + NT)
                act.wait_ge(rsd, b)
                nc.scalar.activation(sd[:, :], mv[:, :, 1], ACT.Sqrt, bias=eps[:, 0:1]).then_inc(sdd, 1)
                act.wait_ge(nbd, b + 1)
                act.wait_ge(h_turned, b * (2 * NI))
                for t in range(NT):
                    nc.scalar.activation(hs[:, t, :], xt[:, b % 2, t, :], ACT.Relu, bias=nb[:, t:t + 1],
                                         scale=rs[:, t:t + 1]).then_inc(h_made, 1)
                layer1_mask(b, 0)
                layer1_mask(b, 1)
                act.wait_ge(hT_out, b * 16)
                for q in range(NI):
                    for kc in range(KC):
                        act.wait_ge(h_turned, b * (2 * NI) + 2 * q + kc + 1)
                        nc.scalar.copy(hT[:, kc, q * IB:(q + 1) * IB], ps_h[:, kc, :]).then_inc(h_saved, 1)

        @block.tensor
        def _(pe):
            pe.wait_ge(consts, 16)
            pe.wait_ge(setup, 3)

            def turn_masks(b, k):
                pe.wait_ge(coded, b * 2 + k + 1)
                for half in range(2):
                    pe.wait_ge(log_made, b * 4)
                    pe.wait_ge(m01_made, b * 4)
                    for j in range(HALF):
                        jt = half * HALF + j
                        mm = pe.transpose(ps_m[:, k, half, j, :], code[:, k, jt * P:(jt + 1) * P], identb[:, :])
                    mm.then_inc(m_turned, 1)

            with pe.Fori(0, B) as b:
                turn_masks(b, 0)
                turn_masks(b, 1)
                for q in range(NI):
                    pe.wait_ge(h_made, b * NT + TI * q + TI)
                    for kc in range(KC):
                        pe.wait_ge(h_saved, b * (2 * NI) + (2 * (q - 1) + kc + 1 if q else 0))
                        for t in range(TI):
                            mm = pe.transpose(ps_h[:, kc, t * P:(t + 1) * P],
                                              hs[:, q * TI + t, kc * P:(kc + 1) * P], ident[:, :])
                        mm.then_inc(h_turned, 1)

        @block.gpsimd
        def _(pool):
            with pool.Fori(0, B) as b:
                for i, (src, made) in enumerate(((rs, rsd), (nb, nbd))):
                    pool.wait_ge(made, b + 1)
                    pass_waits(pool, passed)
                    nc.gpsimd.tensor_copy(hnorm[:, i, bass.ds(b * NT, NT)], src[:, :]).then_inc(norm_kept, 1)
    s.close()


LEAD = 2
ER = 4
TPC = CH // P
RB_STEPS = {3: (0, 1), 4: (2, 3), 5: (4, 5), 6: (6, 7)}
RE = P // (2 * NC)
K_STEP, Q_STEP, V_STEP = 0, 2, 4


def stage_attend(nc, d, ident, mask_log):
    s = Scope(nc)
    wqT, wkT, wvT = (s.sb(n, [P, KC, F]) for n in ("wqT", "wkT", "wvT"))
    bq, bk = s.sb("bq", [P, KC]), s.sb("bk", [P, KC])
    bv = s.sb("bv", [P, F])
    onehot = s.sb("onehot", [P, 4, 32])
    sel = s.sb("sel", [4 * NC, NC, P], F32R)
    hkv = s.sb("hkv", [P, KC, IB])
    hq = s.sb("hq", [P, KC, IB])
    kst = s.sb("kst", [P, KC, 2, N], F32R)
    qst = s.sb("qst", [P, 2, 2, 2, IB], F32R)
    vt = s.sb("vt", [P, KC, NT, P])
    ex = s.sb("ex", [P, ER, TPC, 2, IB])
    pair_sum = s.sb("pair_sum", [P, ER, 2, IB])
    num = s.sb("num", [P, 2, NC, IB])
    wrow = [num[:, 0, m, :].rearrange("p (c f) -> p c f", c=KC) for m in range(3)]
    sel_in = num[0:4 * NC, 0, 3:5, :].rearrange("p a (b e) -> p (a b) e", e=P)
    hkv_first = [hkv[:, :, :]] + [num[:, 1, KC * n:KC * (n + 1), :] for n in range(NI - 1)]
    den = s.sb("den_rows", [P, IB])
    den_t = s.sb("den_t", [P, IB // RE])
    rec_t = s.sb("rec_t", [P, 2, IB // RE], F32R)
    rec = s.sb("rec", [2 * 2 * NC, IB], F32R)
    ctx = s.sb("ctx", [P, IB])

    ps_s = s.ps("ps_s", [P, 2, TPC, IB])
    ps_n = s.ps("ps_n", [P, IB])
    ps_d = s.ps("ps_d", [P, IB])
    ps_r = s.ps("ps_r", [P, IB])
    ps_p = s.ps("ps_p", [P, IB])

    def sems(*names):
        return [s.sem("b_" + n) for n in names]

    w_in, small_in, w_turned, w_saved, sel_made = sems("w", "small", "wt", "ws", "selm")
    kv_in, q_in = sems("kvin", "qin")
    k_proj, q_proj, v_proj, k_hi, q_hi, k_done, q_done, v_done = sems(
        "kproj", "qproj", "vproj", "khi", "qhi", "kdone", "qdone", "vdone")
    scores, clipped, probs, summed = sems("scores", "clip", "probs", "summed")
    num_done, num_saved, den_done, den_saved, den_moved = sems("num", "nsave", "den", "dsave", "dmove")
    inverted, rec_hi, rec_lo, rec_moved, q_twice = sems("inv", "rhi", "rlo", "rmove", "qtwice")
    spread, scaled, added, ctx_out = sems("spread", "scaled", "added", "ctxout")
    bias_made, passed = sems("bias", "passed")
    NBLK = B * KC * NI

    def iterations(e, body):
        def turn(b, pair, refill, last, peel=False):
            base = b * (2 * NI) + pair * NI
            if peel:
                body(e, b, base, base, 0, pair, True, False, refill, True)
            with e.Fori(1 if peel else 0, NI - 1) as ib:
                body(e, b, base, base + ib, ib, pair, False, False, refill, True)
            body(e, b, base, base + NI - 1, NI - 1, pair, False, True, refill, not last)
        turn(0, 0, True, False, peel=True)
        turn(0, 1, True, False)
        with e.Fori(1, B - 1) as b:
            turn(b, 0, True, False)
            turn(b, 1, True, False)
        turn(B - 1, 0, True, False)
        turn(B - 1, 1, False, True)

    def cols(ib):
        return bass.ds(ib * IB, IB)

    def num_slot(it, c):
        return num[:, it % 2, c, :]

    def half(h):
        return slice(h * DH, (h + 1) * DH)

    with nc.Block() as block:

        @block.sync
        def _(sp):
            def load(dst, b, ib, sem):
                sp.dma_start(dst, d["hT"][b][:, :, cols(ib)]).then_inc(sem, 16)

            for m, w in enumerate(("wq", "wk", "wv")):
                sp.dma_start(wrow[m], d[w].rearrange("(c p) f -> p c f", p=P)).then_inc(w_in, 16)
            for ib in range(NI):
                load(hkv_first[ib], 0, ib, kv_in)
            load(hq[:, :, :], 0, 0, q_in)
            for dst, src in ((bq[:, :], d["bq"].rearrange("(c p) -> p c", p=P)),
                             (bk[:, :], d["bk"].rearrange("(c p) -> p c", p=P)),
                             (bv[:, :], d["bv"].partition_broadcast(P)),
                             (onehot[:, :, :], d["onehot"]), (sel_in[:, :, :], d["sel"])):
                sp.dma_start(dst, src, allow_slow_non_contiguous=True).then_inc(small_in, 16)

            def queries_twice(it, par):
                sp.wait_ge(q_done, it + 1)
                for h in range(2):
                    sp.dma_start(qst[half(1 - h), par, h].bitcast(F32), qst[half(h), par, h].bitcast(F32)).then_inc(q_twice, 16)

            def gather(it):
                sp.wait_ge(den_saved, it + 1)
                for q in range(4):
                    sp.dma_start(den_t[q * 32:(q + 1) * 32, :], den[q * 32:q * 32 + NC // 2, :].rearrange(
                        "m (i e) -> m i e", i=RE)).then_inc(den_moved, 16)

            def scatter(it):
                sp.wait_ge(rec_lo, it + 1)
                sp.wait_ge(spread, it * NC)
                for k in range(2):
                    sp.dma_start(rec[k * 2 * NC:(k + 1) * 2 * NC, :].bitcast(F32).rearrange("r (i e) -> r i e", i=RE),
                                 rec_t[:, k, :].bitcast(F32)).then_inc(rec_moved, 16)

            sp.wait_ge(v_proj, NI)
            load(hkv[:, :, :], 0, 0, kv_in)
            queries_twice(0, 0)

            def body(e, b, base, it, ib, pair, first, cross, refill, more):
                if not first:
                    gather(it - 1)
                if more:
                    sp.wait_ge(q_proj, it + 1)
                    pass_waits(sp, passed)
                    nb_, nib = (b + pair, 0) if cross else (b, ib + 1)
                    load(hq[:, :, :], nb_, nib, q_in)
                if not first:
                    scatter(it - 1)
                if more:
                    queries_twice(it + 1, (it + 1) % 2)
                if refill and not (cross and isinstance(b, int) and b == B - 1):
                    sp.wait_ge(v_proj, it + NI + 1)
                    rb, rib = (b + 1, 0) if cross else (b + pair, ib + 1)
                    load(hkv[:, :, :], rb, rib, kv_in)
                if not first:
                    sp.wait_ge(added, it * (NC - 1))
                    sp.dma_start(d["ctxT"][it - 1], ctx[:, :]).then_inc(ctx_out, 16)

            iterations(sp, body)
            gather(NBLK - 1)
            scatter(NBLK - 1)
            sp.wait_ge(added, NBLK * (NC - 1))
            sp.dma_start(d["ctxT"][NBLK - 1], ctx[:, :]).then_inc(ctx_out, 16)
            sp.wait_ge(ctx_out, 16 * NBLK)

        @block.tensor
        def _(pe):
            pe.wait_ge(w_in, 16 * 3)
            for m in range(3):
                if m == 2:
                    pe.wait_ge(w_saved, 1)
                for kc in range(KC):
                    for oc in range(KC):
                        mm = pe.transpose(ps_s[:, m % 2, kc, oc * P:(oc + 1) * P], wrow[m][:, oc, kc * P:(kc + 1) * P],
                                          ident[:, :])
                mm.then_inc(w_turned, 1)
            pe.wait_ge(small_in, 16 * 5)

            def hblock(n):
                return hkv_first[n] if isinstance(n, int) and n < NI else hkv

            def project_k(pair, n):
                if isinstance(n, int) and n < NI:
                    pe.wait_ge(kv_in, NI * 16)
                else:
                    pe.wait_ge(kv_in, n * 16 + 16)
                pe.wait_ge(v_done, n)
                for kc in range(KC):
                    mm = pe.matmul(ps_p[:, :], wkT[:, kc, pair * P:(pair + 1) * P], hblock(n)[:, kc, :],
                                   start=(kc == 0), stop=(kc == KC - 1))
                mm.then_inc(k_proj, 1)

            def project_v(pair, n):
                for t in range(TI):
                    for kc in range(KC):
                        mm = pe.matmul(ps_p[:, t * P:(t + 1) * P], hblock(n)[:, kc, t * P:(t + 1) * P],
                                       wvT[:, kc, pair * P:(pair + 1) * P], start=(kc == 0), stop=(kc == KC - 1))
                mm.then_inc(v_proj, 1)

            def project_q(pair, nit):
                pe.wait_ge(q_in, nit * 16 + 16)
                for kc in range(KC):
                    mm = pe.matmul(ps_p[:, :], wqT[:, kc, pair * P:(pair + 1) * P], hq[:, kc, :],
                                   start=(kc == 0), stop=(kc == KC - 1))
                mm.then_inc(q_proj, 1)

            def score(it, c, h, pair):
                for t in range(TPC):
                    jt = c * TPC + t
                    for half in range(2):
                        mm = pe.matmul(ps_s[:, h, t, :], kst[:, pair, h, jt * P:(jt + 1) * P],
                                       qst[:, it % 2, h, half, :], start=(half == 0), stop=(half == 1))
                mm.then_inc(scores, 1)

            def broadcast(it, c):
                pe.matmul(ps_r[:, :], sel[:, c, :], rec[:, :], start=True, stop=True).then_inc(spread, 1)

            pe.wait_ge(w_saved, 3)
            for n in range(NI):
                project_k(0, n)
                pe.wait_ge(k_done, n + 1)
                project_v(0, n)
            pe.wait_ge(v_done, NI)
            project_q(0, 0)
            pe.wait_ge(q_twice, 32)
            for c in range(LEAD):
                for h in range(2):
                    if c:
                        pe.wait_ge(clipped, 2 * (c - 1) + h + 1)
                    score(0, c, h, 0)

            def body(e, b, base, it, ib, pair, first, cross, refill, more):
                g0 = it * NC
                for c in range(NC):
                    ahead = more or c + LEAD < NC
                    over = c + LEAD >= NC
                    spair = 1 - pair if over and cross else pair
                    if c == NC - LEAD and more:
                        pe.wait_ge(q_twice, it * 32 + 64)
                        if cross:
                            pe.wait_ge(k_done, it + NI + 1)
                    if ahead:
                        pe.wait_ge(clipped, g0 * 2 + 2 * (c + 1) + 1)
                        score(it + 1 if over else it, (c + LEAD) % NC, 0, spair)
                    pe.wait_ge(probs, g0 * 2 + 2 * c + 2)
                    pe.wait_ge(num_saved, g0 + c)
                    if c == 0:
                        pe.wait_ge(v_done, base + NI)
                    for t in range(TPC):
                        for h in range(2):
                            mm = pe.matmul(ps_n[h * DH:(h + 1) * DH, :], vt[:, pair, c * TPC + t, h * DH:(h + 1) * DH],
                                           ex[:, c % ER, t, h, :], start=(t == 0), stop=(t == TPC - 1))
                    mm.then_inc(num_done, 1)
                    if not first and c in RB_STEPS:
                        pe.wait_ge(rec_moved, it * 32)
                        pe.wait_ge(scaled, (it - 1) * NC + RB_STEPS[c][0])
                        broadcast(it - 1, RB_STEPS[c][0])
                    if ahead:
                        pe.wait_ge(clipped, g0 * 2 + 2 * (c + 1) + 2)
                        score(it + 1 if over else it, (c + LEAD) % NC, 1, spair)
                    if c % 2:
                        pe.wait_ge(summed, g0 + c + 1)
                        if c == 1 and not first:
                            pe.wait_ge(den_saved, it)
                        for cc in (c - 1, c):
                            for h in range(2):
                                q = (cc % 2) * 2 + h
                                mm = pe.matmul(ps_d[q * 32:(q + 1) * 32, :], onehot[:, c // 2, :],
                                               pair_sum[:, cc % ER, h, :], start=(c == 1), stop=(c == NC - 1),
                                               tile_position=(0, 32 * q))
                        mm.then_inc(den_done, 1)
                    if c == K_STEP and refill:
                        project_k(1 - pair, it + NI)
                    if c == Q_STEP and more:
                        if refill:
                            pe.wait_ge(k_done, it + NI + 1)
                        else:
                            pe.wait_ge(q_done, it + 1)
                            pe.wait_ge(v_done, NBLK)
                        project_q(1 - pair if cross else pair, it + 1)
                    if c == V_STEP and refill:
                        pe.wait_ge(q_done, it + 2)
                        project_v(1 - pair, it + NI)
                    if not first and c in RB_STEPS:
                        pe.wait_ge(scaled, (it - 1) * NC + RB_STEPS[c][1])
                        broadcast(it - 1, RB_STEPS[c][1])

            iterations(pe, body)
            for c in range(NC):
                if c == 0:
                    pe.wait_ge(rec_moved, NBLK * 32)
                pe.wait_ge(scaled, (NBLK - 1) * NC + c)
                broadcast(NBLK - 1, c)

        @block.vector
        def _(dve):
            for m, (dst, sc) in enumerate(((wqT, DH ** -0.5), (wkT, 1.0), (wvT, 1.0))):
                dve.wait_ge(w_turned, m + 1)
                dve.tensor_scalar(dst[:, :, :], ps_s[:, m % 2, :, 0:F], sc, None, ALU.mult).then_inc(w_saved, 1)
            dve.wait_ge(small_in, 16 * 5)
            dve.tensor_scalar(bq[:, :], bq[:, :], DH ** -0.5, None, ALU.mult).then_inc(bias_made, 1)
            dve.tensor_copy(sel[:, :, :], sel_in[:, :, :]).then_inc(sel_made, 1)
            dve.wait_ge(bias_made, 1)

            def split_k(pair, ib, n):
                for h in range(2):
                    dve.wait_ge(k_hi, n * 2 + 2)
                    last = dve.scalar_tensor_tensor(
                        out=kst[half(1 - h), pair, h, cols(ib)], in0=ps_p[half(h), :], scalar=bk[half(h), pair:pair + 1],
                        in1=kst[half(h), pair, h, cols(ib)].bitcast(F32), op0=ALU.add, op1=ALU.subtract)
                last.then_inc(k_done, 1)

            def split_q(pair, it):
                dve.wait_ge(q_hi, it * 2 + 2)
                for h in range(2):
                    last = dve.scalar_tensor_tensor(
                        out=qst[half(h), it % 2, h, 1, :], in0=ps_p[half(h), :], scalar=bq[half(h), pair:pair + 1],
                        in1=qst[half(h), it % 2, h, 0, :].bitcast(F32), op0=ALU.add, op1=ALU.subtract)
                last.then_inc(q_done, 1)

            def copy_v(pair, ib, n):
                dve.wait_ge(v_proj, n + 1)
                dve.tensor_tensor(vt[:, pair, bass.ds(ib * TI, TI), :], ps_p[:, :].rearrange("p (t e) -> p t e", t=TI),
                                  bv[:, pair * P:(pair + 1) * P].unsqueeze(1).broadcast_to([P, TI, P]),
                                  ALU.add).then_inc(v_done, 1)

            def clip(it, c, h, ib):
                dve.wait_ge(scores, it * (2 * NC) + 2 * c + h + 1)
                dve.scalar_tensor_tensor(out=ex[:, c % ER, :, h, :], in0=ps_s[:, h, :, :], scalar=-LIM,
                                         in1=mask_log[:, c * TPC:(c + 1) * TPC, cols(ib)],
                                         op0=ALU.max, op1=ALU.min).then_inc(clipped, 1)

            def invert(it):
                dve.wait_ge(den_moved, it * 64 + 64)
                dve.reciprocal(den_t[:, :], den_t[:, :]).then_inc(inverted, 1)

            def high_rec(it):
                dve.wait_ge(inverted, it + 1)
                dve.wait_ge(rec_moved, it * 32)
                dve.tensor_copy(rec_t[:, 0, :], den_t[:, :]).then_inc(rec_hi, 1)

            def low_rec(it):
                dve.wait_ge(rec_hi, it + 1)
                dve.tensor_tensor(rec_t[:, 1, :], den_t[:, :], rec_t[:, 0, :].bitcast(F32),
                                  ALU.subtract).then_inc(rec_lo, 1)

            def scale(it, c):
                dve.wait_ge(spread, it * NC + c + 1)
                dve.wait_ge(num_saved, it * NC + c + 1)
                dve.tensor_tensor(num_slot(it, c), ps_r[:, :], num_slot(it, c), ALU.mult).then_inc(scaled, 1)

            for ib in range(NI):
                split_k(0, ib, ib)
                copy_v(0, ib, ib)
            split_q(0, 0)
            for c in range(LEAD):
                for h in range(2):
                    clip(0, c, h, 0)

            def body(e, b, base, it, ib, pair, first, cross, refill, more):
                for c in range(NC):
                    over = c + LEAD >= NC
                    if not over:
                        sit, sib = it, ib
                    else:
                        sit, sib = it + 1, 0 if cross else ib + 1
                    if more or not over:
                        if not (first and c < ER - LEAD):
                            dve.wait_ge(num_done, it * NC + c + LEAD - ER + 1)
                            dve.wait_ge(summed, it * NC + c + LEAD - ER + 1)
                        for h in range(2):
                            clip(sit, (c + LEAD) % NC, h, sib)
                            if h == 0 and not first and c == 1:
                                invert(it - 1)
                            if h == 0 and not first and c == 2:
                                low_rec(it - 1)
                            if h == 0 and not first and c in RB_STEPS:
                                scale(it - 1, RB_STEPS[c][0])
                    elif not first and c in RB_STEPS:
                        scale(it - 1, RB_STEPS[c][0])
                    if not first:
                        if c == 1:
                            high_rec(it - 1)
                        if c in RB_STEPS:
                            scale(it - 1, RB_STEPS[c][1])
                    if c == K_STEP + 1 and refill:
                        split_k(1 - pair, ib, it + NI)
                    if c == Q_STEP + 1 and more:
                        split_q(1 - pair if cross else pair, it + 1)
                    if c == V_STEP + 1 and refill:
                        copy_v(1 - pair, ib, it + NI)

            iterations(dve, body)
            last = NBLK - 1
            invert(last)
            high_rec(last)
            low_rec(last)
            for c in range(NC):
                scale(last, c)

        @block.scalar
        def _(act):
            act.wait_ge(bias_made, 1)

            def high_k(pair, ib, n):
                act.wait_ge(k_proj, n + 1)
                for h in range(2):
                    nc.scalar.activation(kst[half(h), pair, h, cols(ib)], ps_p[half(h), :], ACT.Identity,
                                         bias=bk[half(h), pair:pair + 1]).then_inc(k_hi, 1)

            def high_q(pair, it):
                act.wait_ge(q_proj, it + 1)
                for h in range(2):
                    nc.scalar.activation(qst[half(h), it % 2, h, 0, :], ps_p[half(h), :], ACT.Identity,
                                         bias=bq[half(h), pair:pair + 1]).then_inc(q_hi, 1)

            def exp(it, c, h):
                act.wait_ge(clipped, it * (2 * NC) + 2 * c + h + 1)
                e = ex[:, c % ER, :, h, :]
                nc.scalar.activation(e, e, ACT.Exp).then_inc(probs, 1)

            def save_num(it, c, first):
                act.wait_ge(num_done, it * NC + c + 1)
                if not first:
                    act.wait_ge(added, (it - 1) * (NC - 1))
                nc.scalar.copy(num_slot(it, c), ps_n[:, :]).then_inc(num_saved, 1)

            def save_den(it):
                act.wait_ge(den_done, it * (NC // 2) + NC // 2)
                act.wait_ge(den_moved, it * 64)
                nc.scalar.copy(den[:, :], ps_d[:, :]).then_inc(den_saved, 1)

            for ib in range(NI):
                high_k(0, ib, ib)
            high_q(0, 0)
            for c in range(LEAD):
                for h in range(2):
                    exp(0, c, h)

            def body(e, b, base, it, ib, pair, first, cross, refill, more):
                for c in range(NC):
                    over = c + LEAD >= NC
                    go = more or not over
                    sit = it + 1 if over else it
                    if go:
                        exp(sit, (c + LEAD) % NC, 0)
                    if c == 0 and not first:
                        save_den(it - 1)
                    save_num(it, c, first)
                    if go:
                        exp(sit, (c + LEAD) % NC, 1)
                    if c == K_STEP and refill:
                        high_k(1 - pair, ib, it + NI)
                    if c == Q_STEP and more:
                        high_q(1 - pair if cross else pair, it + 1)

            iterations(act, body)
            save_den(NBLK - 1)

        @block.gpsimd
        def _(pool):
            def pair_up(it, c, fresh=False):
                pool.wait_ge(probs, it * (2 * NC) + 2 * c + 2)
                if not fresh:
                    pool.wait_ge(den_done, it * (NC // 2) + (c - ER) // 2 + 1)
                nc.gpsimd.tensor_tensor(pair_sum[:, c % ER], ex[:, c % ER, 0], ex[:, c % ER, 1],
                                        ALU.add).then_inc(summed, 1)

            def add(it, c):
                if c == 1:
                    pool.wait_ge(scaled, it * NC + 2)
                    pool.wait_ge(ctx_out, it * 16)
                    nc.gpsimd.tensor_tensor(ctx[:, :], num_slot(it, 0), num_slot(it, 1), ALU.add).then_inc(added, 1)
                else:
                    pool.wait_ge(scaled, it * NC + c + 1)
                    pool.wait_ge(added, it * (NC - 1) + c - 1)
                    nc.gpsimd.tensor_tensor(ctx[:, :], ctx[:, :], num_slot(it, c), ALU.add).then_inc(added, 1)

            for c in range(LEAD):
                pair_up(0, c, fresh=True)

            def body(e, b, base, it, ib, pair, first, cross, refill, more):
                for c in range(NC):
                    over = c + LEAD >= NC
                    if more or not over:
                        pair_up(it + 1 if over else it, (c + LEAD) % NC, fresh=first and c < ER - LEAD)
                    if not first:
                        for cc in RB_STEPS.get(c, ()):
                            if cc:
                                add(it - 1, cc)

            iterations(pool, body)
            for c in range(1, NC):
                add(NBLK - 1, c)
    s.close()


WA = F + 2 * H


def stage_between(nc, d, ident, ecol, hnorm):
    s = Scope(nc)
    NBK = B * NI
    worow = s.sb("worow", [P, KC, F])
    woT = s.sb("woT", [P, KC, F])
    waug = s.sb("waug", [P, KC, WA])
    att = s.sb("att", [P, H, 2 * DH])
    wa = s.sb("wa", [P, KC, 2, F])
    gamma, beta, bo_row = s.sb("gamma", [P, F]), s.sb("beta", [P, F]), s.sb("bo_row", [P, F])
    eps = s.sb("c_eps", [P, 1])
    cT = s.sb("cT", [P, 2, KC, IB])
    hbt = s.sb("hbt", [P, 4, TI, F])
    xin = s.sb("xin", [P, 4, TI, F])
    y = s.sb("y", [P, 4, TI, F])
    x1 = s.sb("x1t", [P, 4, TI, F])
    h2 = s.sb("h2", [P, 2, TI, F])
    h2T = s.sb("h2T", [P, 2, KC, IB])
    wh = s.sb("wht", [P, 2, TI, WA])
    er = s.sb("er", [H, 2, IB])
    st = [s.sb(f"c_st{i}", [P, TI, 6]) for i in range(2)]
    mv = [s.sb(f"c_mv{i}", [P, TI, 2]) for i in range(2)]
    sd = [s.sb(f"c_sd{i}", [P, TI]) for i in range(2)]
    rs = [s.sb(f"c_rs{i}", [P, TI]) for i in range(2)]
    nb = [s.sb(f"c_nb{i}", [P, TI]) for i in range(2)]
    ps_y = s.ps("ps_y", [P, TI, F])
    ps_t = s.ps("ps_t", [P, KC, IB])
    ps_w = s.ps("ps_w", [P, 3, IB])
    ps_e = s.ps("ps_e", [H, IB])

    def sems(*names):
        return [s.sem("c_" + n) for n in names]

    wo_in, w_in, wo_turned, setup, wa_made, passed = sems("wo", "w", "wot", "setup", "wa", "passed")
    c_in, x_in, h_made, hb_made = sems("cin", "xin", "h", "hb")
    y_proj, y_made, stat, aggr, sdd, rsd, nbd = sems("yp", "y", "stat", "aggr", "sd", "rs", "nb")
    stat2, aggr2, sdd2, rsd2, nbd2 = sems("stat2", "aggr2", "sd2", "rs2", "nb2")
    normed, scaled, xb_made, x1_made, h2_made, turned, turn_saved = sems("n", "g", "xb", "x1", "h2", "t", "ts")
    wh_proj, wh_saved01, wh_saved23, er_turned, er_saved, ec_saved = sems("whp", "whs01", "whs23", "ert", "ers", "ecs")
    x1_out, wh_out, er_out = sems("x1o", "who", "ero")

    def steps(e, body, tail=0):
        for n in range(6):
            body(n, n % 2, True, n >= 2, n >= 3)
        with e.Fori(3, (NBK - tail) // 2) as m:
            for par in range(2):
                body(m * 2 + par, par, True, True, True)
        for n in range(NBK - tail, NBK + 3):
            body(n, n % 2, n < NBK, n < NBK + 2, True)

    def since(n, first):
        return not isinstance(n, int) or n >= first

    def nodes(ap, n):
        return ap.rearrange("b n f -> (b n) f")[bass.ds(n * IB, IB), :].rearrange("(t p) f -> p t f", p=P)

    with nc.Block() as block:

        @block.sync
        def _(sp):
            sp.dma_start(worow[:, :, :], d["wo"].rearrange("(c p) f -> p c f", p=P)).then_inc(wo_in, 16)

            def loads(n):
                if not isinstance(n, int):
                    pass_waits(sp, passed)
                for q in range(KC):
                    sp.dma_start(cT[:, n % 2, q, :], d["ctxT"][(n // NI) * (KC * NI) + q * NI + n % NI]).then_inc(c_in, 16)
                sp.dma_start(xin[:, n % 4], nodes(d["x"], n)).then_inc(x_in, 16)

            loads(0)
            for kc in range(KC):
                sp.dma_start(waug[:, kc, 0:F].rearrange("p (h e) -> p h e", h=H),
                             d["w1"][:, kc * P:(kc + 1) * P, :].rearrange("h p e -> p h e")).then_inc(w_in, 16)
            for dst, src in ((att[:, :, :], d["a"]), (gamma[:, :], d["gamma"]), (beta[:, :], d["beta"]),
                             (bo_row[:, :], d["bo"])):
                sp.dma_start(dst, src.partition_broadcast(P)).then_inc(w_in, 16)

            def store_er(q, par):
                sp.wait_ge(er_saved, q + 1)
                sp.wait_ge(er_out, q * 16)
                pass_waits(sp, passed)
                sp.dma_start(er_dst(q), er[:, par, :]).then_inc(er_out, 16)

            def body(n, par, s0, s1, s2):
                if s0 and not (isinstance(n, int) and n + 1 >= NBK):
                    sp.wait_ge(c_in, n * 32 + 32)
                    sp.wait_ge(x_in, n * 16 + 16)
                    sp.wait_ge(y_proj, n)
                    if s2:
                        pass_waits(sp, passed)
                        sp.wait_ge(x1_made, n - 2)
                    loads(n + 1)
                if since(n, 4):
                    store_er(n - 4, par)
                if s1:
                    sp.wait_ge(x1_made, n - 1)
                    pass_waits(sp, passed)
                    sp.wait_ge(x1_out, (n - 2) * 16)
                    pass_waits(sp, passed)
                    sp.dma_start(nodes(d["x1"], n - 2), x1[:, (n - 2) % 4]).then_inc(x1_out, 16)
                if s2:
                    sp.wait_ge(wh_saved01, (n - 3) * 2 + 2)
                    pass_waits(sp, passed)
                    sp.wait_ge(wh_saved23, (n - 3) * 2 + 2)
                    pass_waits(sp, passed)
                    sp.wait_ge(wh_out, (n - 3) * 16)
                    pass_waits(sp, passed)
                    sp.dma_start(wh_dst(n - 3), wh[:, 1 - par]).then_inc(wh_out, 16)

            def wh_dst(n):
                return d["wh"][n // NI][:, bass.ds(n % NI * TI, TI), :]

            def er_dst(n):
                return d["er"][n // NI][:, bass.ds(n % NI * IB, IB)]

            steps(sp, body, tail=2)
            store_er(NBK - 1, (NBK - 1) % 2)
            sp.wait_ge(x1_out, 16 * NBK)
            sp.wait_ge(wh_out, 16 * NBK)
            sp.wait_ge(er_out, 16 * NBK)

        @block.tensor
        def _(pe):
            pe.wait_ge(wo_in, 16)
            for kc in range(KC):
                for oc in range(KC):
                    mm = pe.transpose(ps_t[:, kc, oc * P:(oc + 1) * P], worow[:, oc, kc * P:(kc + 1) * P], ident[:, :])
            mm.then_inc(wo_turned, 1)
            pe.wait_ge(setup, 2)

            def body(n, par, s0, s1, s2):
                if s0:
                    pe.wait_ge(c_in, n * 32 + 32)
                    pe.wait_ge(y_made, n)
                    for t in range(TI):
                        for kc in range(KC):
                            mm = pe.matmul(ps_y[:, t, :], cT[:, par, kc, t * P:(t + 1) * P], woT[:, kc, :],
                                           start=(kc == 0), stop=(kc == KC - 1))
                    mm.then_inc(y_proj, 1)
                if s2:
                    q = n - 3
                    pe.wait_ge(turn_saved, (n - 2) * KC)
                    if isinstance(n, int) and n == 3:
                        pe.wait_ge(w_in, 16 * 6)
                        pe.wait_ge(wa_made, 4 * KC)
                    for t in range(TI):
                        if t == 2:
                            pe.wait_ge(wh_saved23, q * 2)
                        else:
                            pe.wait_ge(wh_saved01, q * 2 + (1 if t == 3 else 0))
                        if t == 0:
                            pe.wait_ge(wh_saved23, q * 2)
                        for kc in range(KC):
                            mm = pe.matmul(ps_w[:, t % 3, 0:WA], h2T[:, 1 - par, kc, t * P:(t + 1) * P],
                                           waug[:, kc, :], start=(kc == 0), stop=(kc == KC - 1))
                        mm.then_inc(wh_proj, 1)
                    pe.wait_ge(er_saved, q)
                    for t in range(TI):
                        pe.wait_ge(wh_saved01 if t < 2 else wh_saved23, q * 2 + t % 2 + 1)
                        mm = pe.transpose(ps_e[:, t * P:(t + 1) * P], wh[:, 1 - par, t, F:F + H], ident[:, :])
                    mm.then_inc(er_turned, 1)
                if s1:
                    pe.wait_ge(h2_made, (n - 1) * TI)
                    pe.wait_ge(turn_saved, (n - 2) * KC)
                    for kc in range(KC):
                        for t in range(TI):
                            mm = pe.transpose(ps_t[:, kc, t * P:(t + 1) * P], h2[:, par, t, kc * P:(kc + 1) * P],
                                              ident[:, :])
                        mm.then_inc(turned, 1)

            steps(pe, body)

        @block.vector
        def _(dve):
            dve.memset(eps[:, :], EPS).then_inc(setup, 1)
            dve.wait_ge(wo_turned, 1)
            dve.tensor_copy(woT[:, :, :], ps_t[:, :, 0:F]).then_inc(setup, 1)
            dve.wait_ge(w_in, 16 * 6)
            for j in range(2):
                for kc in range(KC):
                    dve.tensor_tensor(wa[:, kc, j, :].rearrange("p (h e) -> p h e", h=H),
                                      waug[:, kc, 0:F].rearrange("p (h e) -> p h e", h=H),
                                      att[:, :, j * DH:(j + 1) * DH], ALU.mult).then_inc(wa_made, 1)
            dve.wait_ge(wa_made, 4)
            for j in range(2):
                for kc in range(KC):
                    dve.tensor_reduce(waug[:, kc, F + j * H:F + (j + 1) * H],
                                      wa[:, kc, j, :].rearrange("p (h e) -> p h e", h=H), AX.X,
                                      ALU.add).then_inc(wa_made, 1)

            def statistics(i, src, n, ss, sa, readers):
                for sem, v in readers:
                    dve.wait_ge(sem, v)
                pass_waits(dve, passed)
                for t in range(TI):
                    dve.bn_stats(st[i][:, t, :], src[:, t, :]).then_inc(ss, 1)
                dve.wait_ge(ss, n * TI + TI)
                pass_waits(dve, passed)
                for t in range(TI):
                    dve.bn_aggr(mv[i][:, t, :], st[i][:, t, :]).then_inc(sa, 1)

            def invert(i, n, s_sd, s_rs, s_nb, s_read, per):
                dve.wait_ge(s_sd, n + 1)
                dve.wait_ge(s_read, n * per)
                dve.reciprocal(rs[i][:, :], sd[i][:, :]).then_inc(s_rs, 1)
                dve.wait_ge(s_rs, n + 1)
                dve.scalar_tensor_tensor(out=nb[i][:, :], in0=mv[i][:, :, 0], scalar=-1.0, in1=rs[i][:, :],
                                         op0=ALU.mult, op1=ALU.mult).then_inc(s_nb, 1)

            def body(n, par, s0, s1, s2):
                if s1:
                    p = n - 2
                    dve.wait_ge(scaled, n - 1)
                    dve.wait_ge(xb_made, n - 1)
                    if since(n, 6):
                        dve.wait_ge(x1_out, (n - 5) * 16)
                    dve.tensor_tensor(x1[:, p % 4], y[:, p % 4], xin[:, p % 4], ALU.add).then_inc(x1_made, 1)
                    dve.wait_ge(x1_made, n - 1)
                    statistics(1, x1[:, p % 4], p, stat2, aggr2, ((aggr2, p * TI), (nbd2, p), (sdd2, p)))
                    invert(1, n - 2, sdd2, rsd2, nbd2, h2_made, TI)
                if s0:
                    dve.wait_ge(y_proj, n + 1)
                    dve.wait_ge(hb_made, n + 1)
                    if since(n, 4):
                        dve.wait_ge(x1_made, n - 3)
                    dve.tensor_tensor(y[:, n % 4], ps_y[:, :, :], hbt[:, n % 4], ALU.add).then_inc(y_made, 1)
                    dve.wait_ge(y_made, n + 1)
                    statistics(0, y[:, n % 4], n, stat, aggr, ((aggr, n * TI), (nbd, n), (sdd, n)))
                if s2:
                    if since(n, 5):
                        dve.wait_ge(wh_out, (n - 4) * 16)
                        dve.wait_ge(ec_saved, n - 4)
                        dve.wait_ge(er_turned, n - 4)
                    for t in (2, 3):
                        dve.wait_ge(wh_proj, (n - 3) * TI + t + 1)
                        dve.tensor_copy(wh[:, 1 - par, t, :], ps_w[:, t % 3, 0:WA]).then_inc(wh_saved23, 1)
                if s0:
                    invert(0, n, sdd, rsd, nbd, normed, TI)

            steps(dve, body)

        @block.scalar
        def _(act):
            act.wait_ge(setup, 2)

            def root(i, n, s_aggr, s_sd, s_rs):
                act.wait_ge(s_aggr, n * TI + TI)
                act.wait_ge(s_rs, n)
                nc.scalar.activation(sd[i][:, :], mv[i][:, :, 1], ACT.Sqrt, bias=eps[:, 0:1]).then_inc(s_sd, 1)

            def residual(n, tiles):
                if 0 in tiles:
                    act.wait_ge(x_in, n * 16 + 16)
                    if since(n, 5):
                        act.wait_ge(y_made, n - 3)
                    pass_waits(act, passed)
                for t in tiles:
                    nc.scalar.activation(hbt[:, n % 4, t, :], xin[:, n % 4, t, :], ACT.Relu,
                                         bias=hnorm[:, 1, bass.ds(n * TI + t, 1)],
                                         scale=hnorm[:, 0, bass.ds(n * TI + t, 1)]).then_inc(h_made, 1)

            residual(0, (0, 1, 2, 3))

            def body(n, par, s0, s1, s2):
                if s1:
                    p = n - 2
                    root(1, p, aggr2, sdd2, rsd2)
                    act.wait_ge(nbd2, n - 1)
                    if since(n, 3):
                        act.wait_ge(turned, (n - 3) * KC)
                    for t in range(TI):
                        nc.scalar.activation(h2[:, par, t, :], x1[:, p % 4, t, :], ACT.Relu,
                                             bias=nb[1][:, t:t + 1], scale=rs[1][:, t:t + 1]).then_inc(h2_made, 1)
                if s2:
                    if since(n, 5):
                        act.wait_ge(wh_out, (n - 4) * 16)
                        act.wait_ge(ec_saved, n - 4)
                        act.wait_ge(er_turned, n - 4)
                    for t in (0, 1):
                        act.wait_ge(wh_proj, (n - 3) * TI + t + 1)
                        nc.scalar.copy(wh[:, 1 - par, t, :], ps_w[:, t % 3, 0:WA]).then_inc(wh_saved01, 1)
                following = s0 and not (isinstance(n, int) and n + 1 >= NBK)
                if following:
                    residual(n + 1, (0, 1))
                if s0:
                    root(0, n, aggr, sdd, rsd)
                if following:
                    residual(n + 1, (2, 3))
                if s0:
                    act.wait_ge(nbd, n + 1)
                    for t in range(TI):
                        nc.scalar.activation(y[:, n % 4, t, :], y[:, n % 4, t, :], ACT.Identity, bias=nb[0][:, t:t + 1],
                                             scale=rs[0][:, t:t + 1]).then_inc(normed, 1)
                if s2:
                    act.wait_ge(er_turned, n - 2)
                    if since(n, 5):
                        act.wait_ge(er_out, (n - 4) * 16)
                    nc.scalar.copy(er[:, 1 - par, :], ps_e[:, :]).then_inc(er_saved, 1)
                if s1:
                    for kc in range(KC):
                        act.wait_ge(turned, (n - 2) * KC + kc + 1)
                        if since(n, 4):
                            act.wait_ge(wh_proj, (n - 3) * TI)
                        nc.scalar.copy(h2T[:, par, kc, :], ps_t[:, kc, :]).then_inc(turn_saved, 1)

            steps(act, body, tail=2)

        @block.gpsimd
        def _(pool):
            pool.wait_ge(w_in, 16 * 6)

            def row(ap):
                return ap[:, :].unsqueeze(1).broadcast_to([P, TI, F])

            def body(n, par, s0, s1, s2):
                if s0:
                    pool.wait_ge(h_made, n * TI + TI)
                    nc.gpsimd.tensor_tensor(hbt[:, n % 4], hbt[:, n % 4], row(bo_row), ALU.add).then_inc(hb_made, 1)
                if not isinstance(n, int) or 1 <= n <= NBK:
                    pool.wait_ge(normed, n * TI)
                    nc.gpsimd.tensor_tensor(y[:, (n - 1) % 4], y[:, (n - 1) % 4], row(gamma), ALU.mult).then_inc(scaled, 1)
                if s0:
                    nc.gpsimd.tensor_tensor(xin[:, n % 4], xin[:, n % 4], row(beta), ALU.add).then_inc(xb_made, 1)
                if s2:
                    pool.wait_ge(wh_saved01, (n - 2) * 2)
                    pool.wait_ge(wh_saved23, (n - 2) * 2)
                    nc.gpsimd.tensor_copy(ecol[:, bass.ds((n - 3) * TI, TI), :],
                                          wh[:, 1 - par, :, F + H:WA]).then_inc(ec_saved, 1)

            steps(pool, body)
    s.close()


QB = 2 * IB
QT = QB // P
NQ = N // QB
NP8 = NT // NQ
NEG = 1.0 - ALPHA
LIFT = 31.0
FINISH = (6, 9, 12, 15)
FIRST = 2


def stage_graph(nc, d, ident, ecol):
    s = Scope(nc)
    NIT = B * NQ
    m01 = s.sb("m01", [P, NT, N], I8)
    lift = s.sb("lift", [P, 1])
    gmax = s.sb("gmax", [P, B * H])
    gall = s.sb("gall", [P, B * H])
    tau = s.sb("tau", [P, B * NT, H])
    vp = s.sb("vp", [P, B * NT, H])
    whin = s.sb("whin", [P, NP8, WA])
    tree = s.sb("tree", [P, 4, F])
    whsum = s.sb("whsum", [P, 4, F])
    whred = s.sb("whred", [P, F])
    whall = s.sb("whall", [P, F])
    vq = s.sb("vq", [P, 2, NT, H, DH])
    vrep = s.sb("vrep", [P, 2, NT, H, 32])
    rho = s.sb("rho", [P, 2, H, QB])
    pr = s.sb("pr", [P, 2, H, QB])
    ns = s.sb("ns", [P, KC, QB])
    ds = s.sb("ds", [P, QB])
    u = s.sb("u", [P, QT, F])
    den = s.sb("den", [P, QT, H])
    empty = s.sb("empty", [P, QT, H])
    dz = s.sb("dz", [P, QT, H])
    rinv = s.sb("rinv", [P, QT, H])
    eb = s.sb("eb", [P, QT, F])
    xo = s.sb("xo", [P, QT, F])
    ps_n = s.ps("ps_n2", [P, KC, QB])
    ps_d = s.ps("ps_d2", [P, QB])
    ps_t = s.ps("ps_t2", [P, 2, IB])

    def sems(*names):
        return [s.sem("d_" + n) for n in names]

    m_in, m_rest, wh_in, er_in, x1_in, stored = sems("m", "mrest", "whin", "er", "x1", "st")
    lift_set, gm, gr, ed, terms, passed = sems("lift", "gm", "gr", "ed", "terms", "passed")
    vq_made, vrep_made, sum_made, treed, wh_read = sems("vq", "vrep", "sum", "tree", "whr")
    rho_relu, rho_made, pr_made, used = sems("rrelu", "rho", "pr", "used")
    n_done = sems("nd0", "nd1")
    n_saved = sems("ns0", "ns1")
    d_saved, turned, raw = sems("ds", "turn", "raw")
    flagged, inverted, pool_step, mixed, low, expd, elu, out_made = sems(
        "flag", "inv", "ps", "mix", "low", "exp", "elu", "out")

    def iterations(e, body):
        body(0, 0, 0, 0, False)
        body(1, 0, 1, 0, True)

        def batch(b, par):
            with e.Fori(0, NQ) as blk:
                body(b * NQ + blk, b, blk, par, True)
        batch(1, 1)
        with e.Fori(1, B // 2) as bb:
            batch(bb * 2, 0)
            batch(bb * 2 + 1, 1)

    def half(ap):
        return ap.rearrange("(t p) f -> p t f", p=P)

    with nc.Block() as block:

        @block.sync
        def _(sp):
            def load_wh(n):
                if not isinstance(n, int):
                    pass_waits(sp, passed)
                sp.dma_start(whin[:, :, :], d["wh"][n // 2][:, bass.ds(n % 2 * NP8, NP8), :]).then_inc(wh_in, 16)

            def load_er(t, slot):
                if not isinstance(t, int):
                    pass_waits(sp, passed)
                sp.dma_start(rho[:, slot], d["er"][t // NQ][:, bass.ds(t % NQ * QB, QB)].partition_broadcast(P)).then_inc(
                    er_in, 16)

            def node_rows(ap, t):
                return half(ap[t // NQ][bass.ds(t % NQ * QB, QB), :])

            load_er(0, 0)
            sp.dma_start(m01[:, 0:FIRST, :], d["mask01"][:, 0:FIRST, :]).then_inc(m_in, 16)
            load_wh(0)
            sp.dma_start(m01[:, FIRST:NT, :], d["mask01"][:, FIRST:NT, :]).then_inc(m_rest, 16)
            sp.wait_ge(wh_read, 1)
            load_wh(1)
            sp.wait_ge(er_in, 16)

            def epilogue(t):
                sp.wait_ge(out_made, t)
                pass_waits(sp, passed)
                sp.dma_start(xo[:, :, :], node_rows(d["x1"], t)).then_inc(x1_in, 16)
                sp.wait_ge(out_made, t + 1)
                pass_waits(sp, passed)
                sp.dma_start(node_rows(d["out"], t), eb[:, :, :]).then_inc(stored, 16)

            def body(t, b, blk, par, before):
                if before:
                    sp.wait_ge(used, t * NT)
                load_er((t + 1) % NIT, (t + 1) % 2)
                sp.wait_ge(wh_read, t + 2)
                load_wh((t + 2) % NIT)
                if before:
                    epilogue(t - 1)
                sp.wait_ge(er_in, t * 16 + 32)
                pass_waits(sp, passed)

            iterations(sp, body)
            epilogue(NIT - 1)
            sp.wait_ge(stored, 16 * NIT)
            sp.wait_ge(wh_in, 16 * (NIT + 2))

        @block.tensor
        def _(pe):
            pe.wait_ge(terms, 2)

            def turn(t, k):
                pe.wait_ge(n_saved[0], t + 1)
                pe.wait_ge(n_saved[1], t + 1)
                pe.wait_ge(d_saved, t + 1)
                if k >= 2:
                    pe.wait_ge(raw, t * QT + k - 1)
                else:
                    pe.wait_ge(raw, t * QT)
                for j, src in enumerate((ns[:, 0], ns[:, 1], ds)):
                    mm = pe.transpose(ps_t[:, k % 2, j * P:(j + 1) * P], src[:, k * P:(k + 1) * P], ident[:, :])
                mm.then_inc(turned, 1)

            def body(t, b, blk, par, before):
                for jt in range(NT):
                    if jt in (0, NP8):
                        pe.wait_ge(vq_made, b * 2 + 1 + jt // NP8)
                        pe.wait_ge(vrep_made, b * 2 + 1 + jt // NP8)
                    first, last = jt == 0, jt == NT - 1
                    for p in range(KC):
                        pe.wait_ge(pr_made, t * (NT * H) + jt * H + 2 * p + 2)
                        if first:
                            pe.wait_ge(n_saved[p], t)
                        for ih in range(2):
                            for hh in range(2):
                                mm = pe.matmul(ps_n[hh * DH:(hh + 1) * DH, p, ih * IB:(ih + 1) * IB],
                                               vq[:, par, jt, 2 * p + hh, :],
                                               pr[:, jt % 2, 2 * p + hh, ih * IB:(ih + 1) * IB], start=first, stop=last)
                        if last:
                            mm.then_inc(n_done[p], 1)
                    if first:
                        pe.wait_ge(d_saved, t)
                    for ih in range(2):
                        for h in range(H):
                            mm = pe.matmul(ps_d[h * 32:(h + 1) * 32, ih * IB:(ih + 1) * IB], vrep[:, par, jt, h, :],
                                           pr[:, jt % 2, h, ih * IB:(ih + 1) * IB], start=first, stop=last,
                                           tile_position=(0, 32 * h))
                    mm.then_inc(used, 1)
                    if before and 2 <= jt < 2 + QT // 2:
                        turn(t - 1, 2 * (jt - 2))
                        turn(t - 1, 2 * (jt - 2) + 1)

            iterations(pe, body)
            for k in range(QT):
                turn(NIT - 1, k)

        @block.vector
        def _(dve):
            dve.memset(lift[:, :], LIFT).then_inc(lift_set, 1)
            dve.tensor_reduce(gmax[:, :].rearrange("p (b h) -> p b h", h=H),
                              ecol[:, :, :].rearrange("p (b t) h -> p b h t", t=NT), AX.X, ALU.max).then_inc(gm, 1)
            dve.wait_ge(gr, 1)
            dve.tensor_tensor(ecol[:, :, :].rearrange("p (b t) h -> p b t h", t=NT),
                              ecol[:, :, :].rearrange("p (b t) h -> p b t h", t=NT),
                              gall[:, :].rearrange("p (b h) -> p b h", h=H).unsqueeze(2).broadcast_to([P, B, NT, H]),
                              ALU.subtract).then_inc(ed, 1)
            dve.wait_ge(terms, 2)
            dve.wait_ge(m_in, 16)

            def finish_a(t):
                dve.wait_ge(raw, (t + 1) * QT)
                dve.wait_ge(mixed, t)
                dve.tensor_scalar(empty[:, :, :], den[:, :, :], 0.0, None, ALU.is_equal).then_inc(flagged, 1)
                dve.wait_ge(flagged, t * 2 + 1)
                dve.scalar_tensor_tensor(out=dz[:, :, :], in0=empty[:, :, :], scalar=float(N), in1=den[:, :, :],
                                         op0=ALU.mult, op1=ALU.add).then_inc(flagged, 1)
                dve.wait_ge(flagged, t * 2 + 2)
                dve.reciprocal(rinv[:, :, :], dz[:, :, :]).then_inc(inverted, 1)

            def finish_b(t):
                dve.wait_ge(mixed, t + 1)
                dve.tensor_scalar(eb[:, :, :], u[:, :, :], 0.0, None, ALU.min).then_inc(low, 1)

            def finish_c(t):
                dve.wait_ge(expd, t + 1)
                dve.scalar_tensor_tensor(out=eb[:, :, :], in0=u[:, :, :], scalar=0.0, in1=eb[:, :, :],
                                         op0=ALU.max, op1=ALU.add).then_inc(elu, 1)

            def finish_d(t):
                dve.wait_ge(elu, t + 1)
                dve.wait_ge(x1_in, t * 16 + 16)
                dve.scalar_tensor_tensor(out=eb[:, :, :], in0=eb[:, :, :], scalar=-1.0, in1=xo[:, :, :],
                                         op0=ALU.add, op1=ALU.add).then_inc(out_made, 1)

            def body(t, b, blk, par, before):
                dve.wait_ge(rho_made, t + 1)
                for jt in range(NT):
                    if isinstance(t, int) and t == 0 and jt == FIRST:
                        dve.wait_ge(m_rest, 16)
                    if before or jt >= 2:
                        dve.wait_ge(used, t * NT + jt - 1)
                    for h in range(H):
                        dve.scalar_tensor_tensor(out=pr[:, jt % 2, h, :], in0=rho[:, t % 2, h, :],
                                                 scalar=tau[:, b * NT + jt, h:h + 1],
                                                 in1=m01[:, jt, bass.ds(blk * QB, QB)], op0=ALU.max,
                                                 op1=ALU.mult).then_inc(pr_made, 1)
                    if before:
                        if jt in FINISH:
                            (finish_a, finish_b, finish_c, finish_d)[FINISH.index(jt)](t - 1)

            iterations(dve, body)
            finish_a(NIT - 1)
            finish_b(NIT - 1)
            finish_c(NIT - 1)
            finish_d(NIT - 1)

        @block.scalar
        def _(act):
            act.wait_ge(ed, 1)
            act.wait_ge(lift_set, 1)
            nc.scalar.activation(tau[:, :, :], ecol[:, :, :], ACT.Exp, scale=NEG).then_inc(terms, 1)
            nc.scalar.activation(vp[:, :, :], ecol[:, :, :], ACT.Exp, scale=ALPHA, bias=lift[:, 0:1]).then_inc(terms, 1)
            act.wait_ge(terms, 2)

            def replicate(n, par):
                b, hf = n // 2, n % 2
                nc.scalar.copy(vrep[:, par, bass.ds(hf * NP8, NP8), :, :],
                               vp[:, bass.ds(n * NP8, NP8), :].unsqueeze(3).broadcast_to([P, NP8, H, 32])).then_inc(
                                   vrep_made, 1)

            def make_rho(t, n):
                act.wait_ge(er_in, t * 16 + 16)
                for h in range(H):
                    nc.scalar.activation(rho[:, t % 2, h, :], rho[:, t % 2, h, :], ACT.Relu,
                                         bias=gall[:, bass.ds(n // NQ * H + h, 1)]).then_inc(rho_relu, 1)
                act.wait_ge(rho_relu, t * H + H)
                pass_waits(act, passed)
                nc.scalar.activation(rho[:, t % 2], rho[:, t % 2], ACT.Exp, scale=-NEG).then_inc(rho_made, 1)

            def save(t):
                act.wait_ge(turned, t * QT)
                for p in range(KC):
                    act.wait_ge(n_done[p], t + 1)
                    nc.scalar.copy(ns[:, p, :], ps_n[:, p, :]).then_inc(n_saved[p], 1)
                act.wait_ge(used, (t + 1) * NT)
                nc.scalar.copy(ds[:, :], ps_d[:, :]).then_inc(d_saved, 1)

            def take(t):
                act.wait_ge(out_made, t)
                act.wait_ge(inverted, t)
                for k in range(QT):
                    act.wait_ge(turned, t * QT + k + 1)
                    nc.scalar.copy(u[:, k, :], ps_t[:, k % 2, 0:F])
                    nc.scalar.copy(den[:, k, :], ps_t[:, k % 2, F:F + P].rearrange("p (h r) -> p h r", h=H)[:, :, 0]
                                   ).then_inc(raw, 1)

            def exponent(t):
                act.wait_ge(low, t + 1)
                nc.scalar.activation(eb[:, :, :], eb[:, :, :], ACT.Exp).then_inc(expd, 1)

            replicate(0, 0)
            replicate(1, 0)
            make_rho(0, 0)

            def body(t, b, blk, par, before):
                if before:
                    save(t - 1)
                    act.wait_ge(used, (t - 1) * NT)
                replicate((t + 2) % NIT, 1 - par)
                if before:
                    take(t - 1)
                make_rho(t + 1, (t + 1) % NIT)
                if before:
                    exponent(t - 1)

            iterations(act, body)
            save(NIT - 1)
            take(NIT - 1)
            exponent(NIT - 1)

        @block.gpsimd
        def _(pool):
            pool.wait_ge(gm, 1)
            nc.gpsimd.partition_all_reduce(gall[:, :], gmax[:, :], P, bass.bass_isa.ReduceOp.max).then_inc(gr, 1)
            pool.wait_ge(terms, 2)

            def values(k, n, par):
                hf = n % 2
                pool.wait_ge(wh_in, k * 16 + 16)
                nc.gpsimd.tensor_tensor(vq[:, par, bass.ds(hf * NP8, NP8), :, :],
                                        whin[:, :, 0:F].rearrange("p t (h e) -> p t h e", h=H),
                                        vp[:, bass.ds(n * NP8, NP8), :].unsqueeze(3).broadcast_to([P, NP8, H, DH]),
                                        ALU.mult).then_inc(vq_made, 1)
                w = NP8 // 2
                nc.gpsimd.tensor_tensor(tree[:, :, :], whin[:, 0:w, 0:F], whin[:, w:NP8, 0:F], ALU.add).then_inc(wh_read, 1)
                pool.wait_ge(wh_read, k + 1)
                nc.gpsimd.tensor_tensor(tree[:, 0:2, :], tree[:, 0:2, :], tree[:, 2:4, :], ALU.add).then_inc(treed, 1)
                pool.wait_ge(treed, 3 * k + 1)
                nc.gpsimd.tensor_tensor(tree[:, 0, :], tree[:, 0, :], tree[:, 1, :], ALU.add).then_inc(treed, 1)
                pool.wait_ge(treed, 3 * k + 2)
                pass_waits(pool, passed)
                nc.gpsimd.partition_all_reduce(whred[:, :], tree[:, 0, :], P,
                                               bass.bass_isa.ReduceOp.add).then_inc(treed, 1)
                pool.wait_ge(treed, 3 * k + 3)
                nc.gpsimd.tensor_copy(whsum[:, n % 4, :], whred[:, :]).then_inc(sum_made, 1)
                pool.wait_ge(sum_made, k + 1)

            def mix(t):
                pool.wait_ge(inverted, t + 1)
                pool.wait_ge(stored, t * 16)
                nc.gpsimd.tensor_tensor(whall[:, :], whsum[:, t // NQ % 2 * 2, :], whsum[:, t // NQ % 2 * 2 + 1, :],
                                        ALU.add).then_inc(pool_step, 1)
                pool.wait_ge(pool_step, t * 3 + 1)

                def per_head(ap):
                    return ap[:, :, :].unsqueeze(3).broadcast_to([P, QT, H, DH])

                def split(ap):
                    return ap[:, :, :].rearrange("p t (h e) -> p t h e", h=H)

                nc.gpsimd.tensor_tensor(split(eb), whall[:, :].rearrange("p (h e) -> p h e", h=H).unsqueeze(1)
                                        .broadcast_to([P, QT, H, DH]), per_head(empty), ALU.mult).then_inc(pool_step, 1)
                pool.wait_ge(pool_step, t * 3 + 2)
                nc.gpsimd.tensor_tensor(u[:, :, :], u[:, :, :], eb[:, :, :], ALU.add).then_inc(pool_step, 1)
                pool.wait_ge(pool_step, t * 3 + 3)
                nc.gpsimd.tensor_tensor(split(u), split(u), per_head(rinv), ALU.mult).then_inc(mixed, 1)

            values(0, 0, 0)
            values(1, 1, 0)

            def body(t, b, blk, par, before):
                if before:
                    pool.wait_ge(used, (t - 1) * NT)
                if before:
                    mix(t - 1)
                values(t + 2, (t + 2) % NIT, 1 - par)

            iterations(pool, body)
            mix(NIT - 1)
    s.close()


def build(nc, ins, out):
    def scratch(name, shape, dt=F32):
        return nc.dram_tensor(name, shape, dt).ap()

    keep = Scope(nc)
    ident = keep.sb("ident", [P, P])
    ecol = keep.sb("ecol", [P, B * NT, H])
    hnorm = keep.sb("hnorm", [P, 2, B * NT])
    d = dict(
        ins, out=out,
        hT=scratch("s_hT", (B, P, KC, N)),
        mask01=scratch("s_mask01", (P, NT, N), I8),
        ctxT=scratch("s_ctxT", (B * KC * NI, P, IB)), x1=scratch("s_x1", (B, N, F)),
        wh=scratch("s_wh", (B, P, NT, WA)), er=scratch("s_er", (B, H, N)))
    layer0 = Scope(nc)
    mask_log = layer0.sb("mask_log", [P, NT, N], I8)
    stage_prepare(nc, d, ident, mask_log, hnorm)
    stage_attend(nc, d, ident, mask_log)
    layer0.close()
    stage_between(nc, d, ident, ecol, hnorm)
    stage_graph(nc, d, ident, ecol)
    keep.close()


_INS = {"x": "x", "adj": "adj", "L0_gnn_Wq": "wq", "L0_gnn_bq": "bq", "L0_gnn_Wk": "wk", "L0_gnn_bk": "bk",
        "L0_gnn_Wv": "wv", "L0_gnn_bv": "bv", "L0_gnn_Wo": "wo", "L0_gnn_bo": "bo", "L0_gnn_gamma": "gamma",
        "L0_gnn_beta": "beta", "L1_gnn_W": "w1", "L1_gnn_a": "a"}


def constants():
    import numpy as np

    onehot = np.zeros((P, NC // 2, 32), np.float32)
    sel = np.zeros((4 * NC, NC, P), np.float32)
    for m in range(32):
        onehot[:, m % 4, m] = 1.0
    for half in range(2):
        for c in range(NC):
            for h in range(2):
                row = half * 2 * NC + ((c % 2) * 2 + h) * (NC // 2) + c // 2
                sel[row, c, h * DH:(h + 1) * DH] = 1.0
    return {"ident": np.eye(P, dtype=np.float32), "onehot": onehot, "sel": sel}


def kernel(**inputs):
    import numpy as np
    import concourse.bacc as bacc
    from concourse.bass_utils import run_bass_kernel_spmd as run

    nc = bacc.Bacc("TRN2", target_bir_lowering=False, num_devices=1)
    arrays, ins = {}, {}
    for name, a in [(k, np.ascontiguousarray(inputs[i])) for i, k in _INS.items()] + list(constants().items()):
        arrays[f"in_{name}"] = a
        ins[name] = nc.dram_tensor(f"in_{name}", a.shape, mybir.dt.from_np(a.dtype), kind="ExternalInput").ap()
    out = nc.dram_tensor("out_0", (B, N, F), F32, kind="ExternalOutput").ap()
    build(nc, ins, out)
    r = run(nc, [arrays], core_ids=[0])
    return r.results[0]["out_0"]
```
